# Optimizing a Trainium2 kernel written in Bass

```python
import numpy as np
import jax
import jax.numpy as jnp

def _softmax(x, axis=-1):
    return jax.nn.softmax(x, axis=axis)

def _gelu(x):
    return jax.nn.gelu(x, approximate=True)

def _silu(x):
    return jax.nn.silu(x)

def _sigmoid(x):
    return jax.nn.sigmoid(x)

def _layernorm(x, axis=-1, eps=1e-05):
    m = jnp.mean(x, axis=axis, keepdims=True)
    v = jnp.var(x, axis=axis, keepdims=True)
    return (x - m) / jnp.sqrt(v + eps)

def _scatter_add(tgt, idx, src, axis=0):
    return tgt.at[idx].add(src)

def _segment_sum(src, seg, n):
    return jax.ops.segment_sum(src, seg, n)
kernel_name = 'mk_seq_postln_d1_jaxref_r8_bf8295'

def setup_inputs(seed: int=0):
    np.random.seed(seed)
    _w = jnp.asarray

    def _L0_attn_setup():
        import jax, jax.numpy as jnp
        import numpy as np
        B, T, D_MODEL = (2, 256, 256)
        N_HEADS, D_HEAD = (16, 128)
        MAX_SEQ_LEN = 256
        LOGIT_SOFTCAP = 50.0
        EPS = 1e-06

        def precompute_rope(dim, max_seq_len, theta=10000.0):
            freqs = 1.0 / theta ** (np.arange(0, dim, 2, dtype=np.float32) / dim)
            t = np.arange(max_seq_len, dtype=np.float32)
            angles = np.outer(t, freqs)
            return (jnp.asarray(np.cos(angles)), jnp.asarray(np.sin(angles)))

        def rmsnorm(x, w):
            return x * jax.lax.rsqrt(jnp.mean(x * x, axis=-1, keepdims=True) + EPS) * w

        def apply_rope(x, cos, sin):
            n = x.shape[1]
            x1, x2 = (x[..., ::2], x[..., 1::2])
            c = cos[:n][None, :, None, :]
            s = sin[:n][None, :, None, :]
            out = jnp.stack([x1 * c - x2 * s, x1 * s + x2 * c], axis=-1)
            return out.reshape(x.shape)
        key = jax.random.key(seed)
        ks = jax.random.split(key, 6)
        x = jax.random.normal(ks[0], (B, T, D_MODEL), dtype=jnp.float32)
        wq = 0.02 * jax.random.normal(ks[1], (N_HEADS * D_HEAD, D_MODEL), dtype=jnp.float32)
        wk = 0.02 * jax.random.normal(ks[2], (N_HEADS * D_HEAD, D_MODEL), dtype=jnp.float32)
        wv = 0.02 * jax.random.normal(ks[3], (N_HEADS * D_HEAD, D_MODEL), dtype=jnp.float32)
        wo = 0.02 * jax.random.normal(ks[4], (D_MODEL, N_HEADS * D_HEAD), dtype=jnp.float32)
        q_norm_w = jnp.ones((D_HEAD,), dtype=jnp.float32)
        k_norm_w = jnp.ones((D_HEAD,), dtype=jnp.float32)
        rope_cos, rope_sin = precompute_rope(D_HEAD, MAX_SEQ_LEN)
        return {'x': x, 'wq': wq, 'wk': wk, 'wv': wv, 'wo': wo, 'q_norm_w': q_norm_w, 'k_norm_w': k_norm_w, 'rope_cos': rope_cos, 'rope_sin': rope_sin}
    _L0_attn_in = _L0_attn_setup()

    def _L0_ffn_setup():
        import jax, jax.numpy as jnp
        import numpy as np
        B, S, H = (1, 128, 256)
        I = 176
        E = 32
        K = 6
        G = 8
        TG = 3
        NSH = 2
        SCALE = 16.0
        C = 48

        def _moe_forward(x3, gate_w, w_gate_up, w_down, ws_gate_up, ws_down):
            b, s, h = x3.shape
            x = x3.reshape(-1, h)
            T = x.shape[0]
            logits = x @ gate_w.T
            grouped = logits.reshape(T, G, E // G)
            group_scores = jnp.max(grouped, axis=-1)
            _, group_idx = jax.lax.top_k(group_scores, TG)
            group_keep = jnp.zeros((T, G), bool).at[jnp.arange(T)[:, None], group_idx].set(True)
            masked = jnp.where(group_keep[..., None], grouped, 0.0)
            scores = masked.reshape(T, E)
            probs = jax.nn.softmax(scores.astype(jnp.float32), axis=-1)
            topk_w, topk_idx = jax.lax.top_k(probs, K)
            topk_w = topk_w * SCALE
            flat_e = topk_idx.reshape(-1)
            tok_idx = jnp.repeat(jnp.arange(T), K)
            oh = jax.nn.one_hot(flat_e, E, dtype=jnp.int32)
            pos = jnp.take_along_axis(jnp.cumsum(oh, axis=0) - 1, flat_e[:, None], axis=1)[:, 0]
            valid = pos < C
            slot = jnp.where(valid, flat_e * C + pos, E * C)
            buf = jnp.zeros((E * C + 1, h), x.dtype).at[slot].set(x[tok_idx])
            xb = buf[:E * C].reshape(E, C, h)
            gu = jnp.einsum('ech,ehf->ecf', xb, w_gate_up)
            g, u = jnp.split(gu, 2, axis=-1)
            act = jax.nn.silu(g) * u
            yb = jnp.einsum('eci,eih->ech', act, w_down)
            yflat = jnp.concatenate([yb.reshape(E * C, h), jnp.zeros((1, h), yb.dtype)], axis=0)
            y_pairs = yflat[slot].reshape(T, K, h)
            out = jnp.einsum('tk,tkh->th', topk_w.astype(x.dtype), y_pairs)
            gu_s = x @ ws_gate_up
            gs, us = jnp.split(gu_s, 2, axis=-1)
            out = out + jax.nn.silu(gs) * us @ ws_down
            return out.reshape(b, s, h)
        key = jax.random.key(seed)
        ks = jax.random.split(key, 6)
        s = 0.02
        return {'hidden_states': jax.random.normal(ks[0], (B, S, H), jnp.float32), 'gate_w': jax.random.normal(ks[1], (E, H), jnp.float32) * s, 'w_gate_up': jax.random.normal(ks[2], (E, H, 2 * I), jnp.float32) * s, 'w_down': jax.random.normal(ks[3], (E, I, H), jnp.float32) * s, 'ws_gate_up': jax.random.normal(ks[4], (H, 2 * I * NSH), jnp.float32) * s, 'ws_down': jax.random.normal(ks[5], (I * NSH, H), jnp.float32) * s}
    _L0_ffn_in = _L0_ffn_setup()
    _d = {'L0_attn_x': _L0_attn_in['x'], 'L0_attn_wq': _L0_attn_in['wq'], 'L0_attn_wk': _L0_attn_in['wk'], 'L0_attn_wv': _L0_attn_in['wv'], 'L0_attn_wo': _L0_attn_in['wo'], 'L0_attn_q_norm_w': _L0_attn_in['q_norm_w'], 'L0_attn_k_norm_w': _L0_attn_in['k_norm_w'], 'L0_attn_rope_cos': _L0_attn_in['rope_cos'], 'L0_attn_rope_sin': _L0_attn_in['rope_sin'], 'L0_ffn_gate_w': _L0_ffn_in['gate_w'], 'L0_ffn_w_gate_up': _L0_ffn_in['w_gate_up'], 'L0_ffn_w_down': _L0_ffn_in['w_down'], 'L0_ffn_ws_gate_up': _L0_ffn_in['ws_gate_up'], 'L0_ffn_ws_down': _L0_ffn_in['ws_down']}
    _x0 = _d['L0_attn_x']
    _d['L0_attn_x'] = jax.random.normal(jax.random.fold_in(jax.random.key(seed), 1), (2, 1024, 256), dtype=_x0.dtype)
    del _x0
    return _d

def reference(L0_attn_x, L0_attn_wq, L0_attn_wk, L0_attn_wv, L0_attn_wo, L0_attn_q_norm_w, L0_attn_k_norm_w, L0_attn_rope_cos, L0_attn_rope_sin, L0_ffn_gate_w, L0_ffn_w_gate_up, L0_ffn_w_down, L0_ffn_ws_gate_up, L0_ffn_ws_down):

    def _L0_attn_ref(x, wq, wk, wv, wo, q_norm_w, k_norm_w, rope_cos, rope_sin):
        import jax, jax.numpy as jnp
        import numpy as np
        B, T, D_MODEL = (2, 256, 256)
        N_HEADS, D_HEAD = (16, 128)
        MAX_SEQ_LEN = 256
        LOGIT_SOFTCAP = 50.0
        EPS = 1e-06

        def precompute_rope(dim, max_seq_len, theta=10000.0):
            freqs = 1.0 / theta ** (np.arange(0, dim, 2, dtype=np.float32) / dim)
            t = np.arange(max_seq_len, dtype=np.float32)
            angles = np.outer(t, freqs)
            return (jnp.asarray(np.cos(angles)), jnp.asarray(np.sin(angles)))

        def rmsnorm(x, w):
            return x * jax.lax.rsqrt(jnp.mean(x * x, axis=-1, keepdims=True) + EPS) * w

        def apply_rope(x, cos, sin):
            n = x.shape[1]
            x1, x2 = (x[..., ::2], x[..., 1::2])
            c = cos[:n][None, :, None, :]
            s = sin[:n][None, :, None, :]
            out = jnp.stack([x1 * c - x2 * s, x1 * s + x2 * c], axis=-1)
            return out.reshape(x.shape)
        Bx, Tx, _ = x.shape
        scale = D_HEAD ** (-0.5)
        q = (x @ wq.T).reshape(Bx, Tx, N_HEADS, D_HEAD).transpose(0, 2, 1, 3)
        k = (x @ wk.T).reshape(Bx, Tx, N_HEADS, D_HEAD).transpose(0, 2, 1, 3)
        v = (x @ wv.T).reshape(Bx, Tx, N_HEADS, D_HEAD).transpose(0, 2, 1, 3)
        q = rmsnorm(q, q_norm_w)
        k = rmsnorm(k, k_norm_w)
        q = apply_rope(q, rope_cos, rope_sin)
        k = apply_rope(k, rope_cos, rope_sin)
        scores = jnp.einsum('bhtd,bhsd->bhts', q, k) * scale
        scores = LOGIT_SOFTCAP * jnp.tanh(scores / LOGIT_SOFTCAP)
        mask = jnp.triu(jnp.ones((Tx, Tx), dtype=bool), k=1)
        scores = jnp.where(mask[None, None], -jnp.inf, scores)
        attn = jax.nn.softmax(scores, axis=-1)
        out = jnp.einsum('bhts,bhsd->bhtd', attn, v)
        out = out.transpose(0, 2, 1, 3).reshape(Bx, Tx, N_HEADS * D_HEAD)
        return out @ wo.T

    def _L0_ffn_ref(hidden_states, gate_w, w_gate_up, w_down, ws_gate_up, ws_down):
        import jax, jax.numpy as jnp
        import numpy as np
        B, S, H = (1, 128, 256)
        I = 176
        E = 32
        K = 6
        G = 8
        TG = 3
        NSH = 2
        SCALE = 16.0
        C = 48

        def _moe_forward(x3, gate_w, w_gate_up, w_down, ws_gate_up, ws_down):
            b, s, h = x3.shape
            x = x3.reshape(-1, h)
            T = x.shape[0]
            logits = x @ gate_w.T
            grouped = logits.reshape(T, G, E // G)
            group_scores = jnp.max(grouped, axis=-1)
            _, group_idx = jax.lax.top_k(group_scores, TG)
            group_keep = jnp.zeros((T, G), bool).at[jnp.arange(T)[:, None], group_idx].set(True)
            masked = jnp.where(group_keep[..., None], grouped, 0.0)
            scores = masked.reshape(T, E)
            probs = jax.nn.softmax(scores.astype(jnp.float32), axis=-1)
            topk_w, topk_idx = jax.lax.top_k(probs, K)
            topk_w = topk_w * SCALE
            flat_e = topk_idx.reshape(-1)
            tok_idx = jnp.repeat(jnp.arange(T), K)
            oh = jax.nn.one_hot(flat_e, E, dtype=jnp.int32)
            pos = jnp.take_along_axis(jnp.cumsum(oh, axis=0) - 1, flat_e[:, None], axis=1)[:, 0]
            valid = pos < C
            slot = jnp.where(valid, flat_e * C + pos, E * C)
            buf = jnp.zeros((E * C + 1, h), x.dtype).at[slot].set(x[tok_idx])
            xb = buf[:E * C].reshape(E, C, h)
            gu = jnp.einsum('ech,ehf->ecf', xb, w_gate_up)
            g, u = jnp.split(gu, 2, axis=-1)
            act = jax.nn.silu(g) * u
            yb = jnp.einsum('eci,eih->ech', act, w_down)
            yflat = jnp.concatenate([yb.reshape(E * C, h), jnp.zeros((1, h), yb.dtype)], axis=0)
            y_pairs = yflat[slot].reshape(T, K, h)
            out = jnp.einsum('tk,tkh->th', topk_w.astype(x.dtype), y_pairs)
            gu_s = x @ ws_gate_up
            gs, us = jnp.split(gu_s, 2, axis=-1)
            out = out + jax.nn.silu(gs) * us @ ws_down
            return out.reshape(b, s, h)
        return _moe_forward(hidden_states, gate_w, w_gate_up, w_down, ws_gate_up, ws_down)
    x = L0_attn_x
    x = _layernorm(x + _L0_attn_ref(x, L0_attn_wq, L0_attn_wk, L0_attn_wv, L0_attn_wo, L0_attn_q_norm_w, L0_attn_k_norm_w, L0_attn_rope_cos, L0_attn_rope_sin), axis=-1)
    x = _layernorm(x + _L0_ffn_ref(x, L0_ffn_gate_w, L0_ffn_w_gate_up, L0_ffn_w_down, L0_ffn_ws_gate_up, L0_ffn_ws_down), axis=-1)
    return x

_drawn_inputs = setup_inputs


def setup_inputs(seed=0):
    import zlib

    import numpy as np

    out = dict(_drawn_inputs(seed))
    spreads = {'L0_attn_q_norm_w': (1.0, 0.6), 'L0_attn_k_norm_w': (1.0, 0.6)}
    factors = {'L0_attn_rope_cos': 3.655,
     'L0_attn_rope_sin': 3.084,
     'L0_ffn_gate_w': 3.182,
     'L0_ffn_ws_gate_up': 2.844,
     'L0_ffn_ws_down': 2.852}
    for name, (base, spread) in spreads.items():
        noise = np.random.default_rng([zlib.crc32(name.encode()), seed]).standard_normal(out[name].shape)
        drawn = base * np.exp(spread * noise) if base else spread * noise
        out[name] = jnp.asarray(drawn.astype(out[name].dtype))
    for name, factor in factors.items():
        out[name] = (out[name] * factor).astype(out[name].dtype)
    return out
```

```python
import numpy as np
import concourse.bass as bass
from concourse import mybir
from concourse.alu_op_type import AluOpType as ALU
from contextlib import ExitStack

F32 = mybir.dt.float32
BF16 = mybir.dt.bfloat16
I32 = mybir.dt.int32
ACT = mybir.ActivationFunctionType
AX = mybir.AxisListType.X

P = 128
B, T, D = 2, 1024, 256
H, DH = 16, 128
N = B * T
NT = N // P
TT = T // P
KC = D // P
CAP = 50.0
RMS_EPS, LN_EPS = 1e-6, 1e-5
E, G, TOPG, TOPK, C = 32, 8, 3, 6, 48
EG = E // G
FI = 176
FH = FI // 2
SI = 2 * FI
SFC = [(0, 128), (128, 128), (256, 96)]
ROUTE_SCALE = 16.0
SLOTS = E * C
SC = SLOTS // P
EB = 8
ECH = EB * C // P
NEG = -3.0e38
POS = 3.0e38

POFF = [sum(T - P * i for i in range(j)) for j in range(TT)]
PLEN = sum(T - P * i for i in range(TT))

SHARED_UNITS = N // 512 * len(SFC)
SHARED_FIRST = 6

UNITS = 24
PROJ = [0, 7]
SSQ = [6, 13]
SUMS = [14, 19]
OUTP = [15, 20]
PJ = 6


def block_kernel(nc, x, xT_d, wqkv_d, wo_d, qn, kn, cos_d, sin_d, gw_d, wgu_d, wd_d, wsgu_d, wsd_d, out):
    rq_d = nc.dram_tensor("rq_rows", (B, T), F32, kind="Internal").ap()
    x1_d = nc.dram_tensor("x1_rows", (N, D), F32, kind="Internal").ap()

    ctx = ExitStack()
    with ctx:
        def sb(name, shape, dt=F32):
            return ctx.enter_context(nc.sbuf_tensor(name, shape, dt))

        def sem(name):
            return ctx.enter_context(nc.semaphore(name))

        yacc = sb("yacc", [P, NT, D])
        ones = sb("ones", [P, 1])
        zero = sb("zero", [P, 1])
        wgu = sb("wgu", [P, EB, KC, 2 * FI])
        wd = sb("wd", [FH, EB, 2, D])
        REGION = 32100
        region = sb("region", [P, REGION])
        at = [0]

        def part(words, reset=None):
            if reset is not None:
                at[0] = reset
            lo = at[0]
            at[0] += words
            assert at[0] <= REGION, at[0]
            return region[:, lo:lo + words]

        xT = part(KC * N, 0).rearrange("p (c n) -> p c n", c=KC)
        wqkv = part(3 * KC * DH).rearrange("p (m c d) -> p m c d", m=3, c=KC)
        wo = part(D)
        probs = [part(PLEN) for _ in range(B)]
        pacc = [part(T) for _ in range(B)]
        qraw = [part(T) for _ in range(B)]
        qhat = [part(T) for _ in range(B)]
        kT = [part(T) for _ in range(B)]
        vS = [part(T).rearrange("p (j d) -> p j d", j=TT) for _ in range(B)]
        rqB = [part(T) for _ in range(B)]
        oT = [part(T) for _ in range(B)]
        qsq, ksq = part(T), part(T)
        var = [part(2 * TT) for _ in range(B)]
        rstd = [part(2 * TT) for _ in range(B)]
        rsum = [part(TT) for _ in range(B)]
        ghead = part(H)
        gcur = part(2)[:, 0:1]
        gtmp = part(4 * H).rearrange("p (k h) -> p k h", k=4)
        nrm = part(4).rearrange("p (k o) -> p k o", o=1)
        causal = sb("causal", [P, P])
        mhalf = sb("mhalf", [P, 2 * TT])

        x1T = part(KC * N, 0).rearrange("p (c n) -> p c n", c=KC)
        gwT = part(KC * E).rearrange("p (c e) -> p c e", c=KC)
        wsgu = part(KC * 2 * SI).rearrange("p (c f) -> p c f", c=KC)
        wsd = part(3 * D).rearrange("p (c n) -> p c n", c=3)
        actS = part(3 * N).rearrange("p (c n) -> p c n", c=3)
        sil = [part(512) for _ in range(2)]
        xbT = part(KC * SLOTS).rearrange("p (c s) -> p c s", c=KC)
        xg0 = at[0]
        xg = part(SC * D).rearrange("p (m d) -> p m d", m=SC)
        sh0 = at[0]
        onehot = part(NT * SLOTS // 2).bitcast(BF16).rearrange("p (i s) -> p i s", i=NT)
        ohT = [part(SLOTS, sh0).rearrange("p (m t) -> p m t", m=SC), part(SLOTS).rearrange("p (m t) -> p m t", m=SC)]
        ybuf = part(SC * D).rearrange("p (m d) -> p m d", m=SC)
        ye = part(4 * D).rearrange("p (r d) -> p r d", r=4)
        silE = part(4 * 2 * C).rearrange("p (r k c) -> p r k c", r=4, k=2)
        actE = part(4 * 2 * C).rearrange("p (r k c) -> p r k c", r=4, k=2)
        at[0] = max(at[0], sh0 + NT * SLOTS // 2)
        rt = [xg0]

        def early(w):
            lo = rt[0]
            rt[0] += NT * w
            assert rt[0] <= xg0 + SC * D
            return region[:, lo:lo + NT * w].rearrange("p (i w) -> p i w", i=NT)

        lg = early(E)
        mk = early(E + 2)
        mrep = early(E + 2)
        wts = sb("wts", [P, NT, E])
        grp = early(G + 5)
        grep = early(G + 5)
        keep = sb("keep", [P, NT, G])
        m8 = sb("m8", [P, NT, 8])
        t8 = sb("t8", [P, NT, 8])
        srow = sb("srow", [P, NT])
        rrow = sb("rrow", [P, NT])
        sel = sb("sel", [P, NT, E], BF16)
        selcum = sb("selcum", [P, NT, E], BF16)
        posm = sb("posm", [P, NT, E])
        NI = 3 * E + 4
        info = sb("info", [P, NT, NI], BF16)
        wrest = sb("wrest", [P, NT, E])
        iota48 = sb("iota48", [P, C])
        iota128 = sb("iota128", [P, P])
        tokloc = sb("tokloc", [P, NT])
        tri = sb("tri", [P, P], BF16)
        onesb = sb("onesb", [P, P], BF16)
        ident = sb("ident", [P, P])
        slot = sb("slot", [P, SC, NI])
        emask = sb("emask", [P, SC, E])
        wsl = sb("wsl", [P, SC, E])
        wslot = sb("wslot", [P, SC])
        tok = sb("tok", [P, SC])
        tokc = sb("tokc", [P, NT, SC])
        toki = sb("toki", [P, SC], I32)
        tokr = sb("tokr", [P, 2, SC])
        stats = sb("stats", [P, NT, 6])
        mv = sb("mv", [P, NT, 2])
        lnv = sb("lnv", [P, NT])
        lnr = sb("lnr", [P, NT])

        ps = ctx.enter_context(nc.psum_tensor("ps", [P, 8, 512], F32))

        x_in, xT_in = sem("x_in"), sem("xT_in")
        small_in, w_in, wo_in = sem("small_in"), sem("w_in"), sem("wo_in")
        consts, g_done, gcur_done = sem("consts"), sem("g_done"), sem("gcur_done")
        pj_done, pj_free = sem("pj_done"), sem("pj_free")
        sq_done, r_done, rq_out, rqB_in = sem("sq_done"), sem("r_done"), sem("rq_out"), sem("rqB_in")
        qhat_done, s_ready, tanh_done = sem("qhat_done"), sem("s_ready"), sem("tanh_done")
        exp_done, mask_done, pacc_done = sem("exp_done"), sem("mask_done"), sem("pacc_done")
        o_ready, o_evac = sem("o_ready"), sem("o_evac")
        dstep = sem("dstep")
        var1, rln1 = sem("var1"), sem("rln1")
        moe_in, x1_out = sem("moe_in"), sem("x1_out")
        rot_done, rot_free = sem("rot_done"), sem("rot_free")
        logit_done, logit_read = sem("logit_done"), sem("logit_read")
        diff_done, e_done, sel_done = sem("diff_done"), sem("e_done"), sem("sel_done")
        pos_done, onehot_done = sem("pos_done"), sem("onehot_done")
        gu_done, sil_done, act_done = sem("gu_done"), sem("sil_done"), sem("act_done")
        tok_done = sem("tok_done")
        xg_in = [sem(f"xg_in{q}") for q in range(3)]
        ew_in = [sem(f"ew_in{k}") for k in range(EB)]
        egu_done, esil_done, eact_done = sem("egu_done"), sem("esil_done"), sem("eact_done")
        ey_done, ey_evac = sem("ey_done"), sem("ey_evac")
        yb_in = [sem(f"yb_in{k}") for k in range(4)]
        oht_done, comb_done, comb_free = sem("oht_done"), sem("comb_done"), sem("comb_free")
        yw_done, var2, rln2, norm_done, out_done = sem("yw_done"), sem("var2"), sem("rln2"), sem("norm_done"), sem("out_done")

        block = ctx.enter_context(nc.Block())
        x_v = x.rearrange("(i p) d -> p i d", p=P)
        x1_v = x1_d.rearrange("(i p) d -> p i d", p=P)
        out_v = out.rearrange("(i p) d -> p i d", p=P)
        wgu_v = wgu_d.rearrange("e (c p) f -> e p c f", p=P)
        wd_v = wd_d.rearrange("e (c p) n -> e p c n", p=FH)

        def expert_pieces(k):
            lo, hi = k * C, (k + 1) * C
            out_, r = [], lo
            while r < hi:
                n = min(hi, (r // P + 1) * P) - r
                out_.append((r - lo, r % P, r // P, n))
                r += n
            return out_

        @block.sync
        def _(sp):
            sp.dma_start(xT, xT_d.rearrange("(c p) n -> p c n", p=P)).then_inc(xT_in, 16)
            sp.dma_start(wqkv, wqkv_d[0]).then_inc(w_in, 16)
            sp.dma_start(gtmp[:, 0, :], cos_d).then_inc(small_in, 16)
            sp.dma_start(gtmp[:, 1, :], sin_d).then_inc(small_in, 16)
            sp.dma_start(nrm[:, 0, :], qn).then_inc(small_in, 16)
            sp.dma_start(nrm[:, 1, :], kn).then_inc(small_in, 16)
            sp.dma_start(wo, wo_d[0]).then_inc(wo_in, 16)
            sp.dma_start(yacc[:, :, :], x_v).then_inc(x_in, 16)
            for k in range(EB):
                sp.dma_start(wgu[:, k], wgu_v[k]).then_inc(ew_in[k], 16)
                sp.dma_start(wd[:, k], wd_v[k]).then_inc(ew_in[k], 16)

            def rq_broadcast(h, b):
                sp.wait_ge(r_done, h * B + b + 1)
                sp.dma_start(rq_d[b].rearrange("(p j) -> p j", p=P), rstd[b][:, 0:TT]).then_inc(rq_out, 16)
                sp.wait_ge(rq_out, h * (16 * B) + 16 * (b + 1))
                sp.dma_start(rqB[b], rq_d[b:b + 1, :].to_broadcast([P, T])).then_inc(rqB_in, 16)

            with sp.Fori(0, H - 1) as h:
                rq_broadcast(h, 0)
                rq_broadcast(h, 1)
                sp.dma_start(wqkv, wqkv_d[bass.ds(h + 1, 1)].rearrange("o p m c d -> p (o m) c d")).then_inc(w_in, 16)
                sp.wait_ge(pj_done, h * UNITS + UNITS)
                sp.dma_start(wo, wo_d[bass.ds(h + 1, 1)].rearrange("o p n -> p (o n)")).then_inc(wo_in, 16)
            rq_broadcast(H - 1, 0)
            rq_broadcast(H - 1, 1)

            sp.wait_ge(pj_free, H * UNITS + 1)
            sp.dma_start(gwT, gw_d.rearrange("(c p) e -> p c e", p=P)).then_inc(moe_in, 16)
            sp.dma_start(wsgu, wsgu_d.rearrange("(c p) f -> p c f", p=P)).then_inc(moe_in, 16)
            for c, (f0, fn) in enumerate(SFC):
                sp.dma_start(wsd[0:fn, c, :], wsd_d[f0:f0 + fn, :]).then_inc(moe_in, 16)
            sp.wait_ge(norm_done, 1)
            sp.dma_start(x1_v, yacc[:, :, :]).then_inc(x1_out, 16)
            with sp.Fori(0, E // EB - 1) as g:
                for k in range(EB):
                    sp.wait_ge(ey_done, g * EB + k + 1)
                    sp.dma_start(wgu[:, k], wgu_v[bass.ds(g * EB + (EB + k), 1)].rearrange("o p c f -> p (o c) f")).then_inc(ew_in[k], 16)
                    sp.dma_start(wd[:, k], wd_v[bass.ds(g * EB + (EB + k), 1)].rearrange("o p c n -> p (o c) n")).then_inc(ew_in[k], 16)
            sp.wait_ge(out_done, 16 * NT)

        @block.tensor
        def _(pe):
            mm = nc.tensor.matmul
            pe.wait_ge(xT_in, 16)
            pe.wait_ge(consts, 2)
            with pe.Fori(0, H) as h:
                def unit(k):
                    pe.wait_ge(pj_free, h * UNITS + max(k - 1, 0) + 1)
                    return ps[:, PJ + k % 2, :]

                def project(b):
                    k = PROJ[b]
                    for m in (0, 1):
                        for half in range(2):
                            bank = unit(k)
                            t0 = b * T + 512 * half
                            for c in range(KC):
                                last = mm(bank, wqkv[:, m, c, :], xT[:, c, t0:t0 + 512], start=c == 0, stop=c == KC - 1)
                            last.then_inc(pj_done, 1)
                            k += 1
                    for half in range(2):
                        bank = unit(k)
                        for j in range(4):
                            t0 = b * T + 512 * half + P * j
                            for c in range(KC):
                                last = mm(bank[:, P * j:P * j + P], xT[:, c, t0:t0 + P], wqkv[:, 2, c, :],
                                          start=c == 0, stop=c == KC - 1)
                        last.then_inc(pj_done, 1)
                        k += 1

                def sums_of_squares(b):
                    bank = unit(SSQ[b])
                    pe.wait_ge(sq_done, h * (2 * B) + 2 * (b + 1))
                    for j in range(TT):
                        mm(bank[:, j:j + 1], qsq.rearrange("d (p j) -> d j p", j=TT)[:, j, :], ones[:, 0:1], start=True, stop=True)
                    for j in range(TT):
                        last = mm(bank[:, TT + j:TT + j + 1], ksq[:, P * j:P * j + P], ones[:, 0:1], start=True, stop=True)
                    last.then_inc(pj_done, 1)

                def scores(b, j):
                    pe.wait_ge(tanh_done, h * (B * TT) + max(b * TT + j - 1, 0) + 1)
                    buf = ps[:, 2 * (j % 2):2 * (j % 2) + 2, :].rearrange("p k n -> p (k n)")
                    for t0, t1 in ([(P * j, 512), (512, T)] if j < 4 else [(P * j, T)]):
                        last = mm(buf[:, t0:t1], kT[b][:, P * j:P * j + P], qhat[b][:, t0:t1], start=True, stop=True)
                    last.then_inc(s_ready, 1)

                def values(b, j):
                    if j == 0:
                        pe.wait_ge(o_evac, h * B + b + 1)
                    pe.wait_ge(mask_done, h * (B * TT) + b * TT + j + 1)
                    o = ps[:, 4:6, :].rearrange("p k n -> p (k n)")
                    for t0, t1 in ([(P * j, 512), (512, T)] if j < 4 else [(P * j, T)]):
                        o0 = POFF[j] + t0 - P * j
                        last = mm(o[:, t0:t1], vS[b][:, j, :], probs[b][:, o0:o0 + t1 - t0],
                                  start=j == 0, stop=(j == 3 and t1 == 512) or j == TT - 1)
                    if j == TT - 1:
                        last.then_inc(o_ready, 1)

                def finish(b):
                    bank = unit(SUMS[b])
                    pe.wait_ge(pacc_done, h * (B * TT) + (b + 1) * TT)
                    for j in range(TT):
                        last = mm(bank[:, j:j + 1], pacc[b][:, P * j:P * j + P], ones[:, 0:1], start=True, stop=True)
                    last.then_inc(pj_done, 1)
                    pe.wait_ge(o_evac, h * B + b + 2)
                    for u in range(4):
                        bank = unit(OUTP[b] + u)
                        for s in range(2):
                            last = mm(bank[:, D * s:D * s + D], oT[b][:, P * (2 * u + s):P * (2 * u + s) + P], wo, start=True, stop=True)
                        last.then_inc(pj_done, 1)

                pe.wait_ge(w_in, h * 16 + 16)
                project(0)
                sums_of_squares(0)
                project(1)
                sums_of_squares(1)
                for b in range(B):
                    pe.wait_ge(qhat_done, h * B + b + 2)
                    for j in range(TT):
                        scores(b, j)
                        if j >= 2:
                            values(b, j - 2)
                        if b == 1 and j == 2:
                            pe.wait_ge(wo_in, h * 16 + 16)
                            finish(0)
                    values(b, TT - 2)
                    values(b, TT - 1)
                finish(1)

            def rot(n):
                if n >= 2:
                    pe.wait_ge(rot_free, n - 1)
                return ps[:, n % 2, :]

            pe.wait_ge(norm_done, 1)
            pe.wait_ge(moe_in, 16 * 5)
            for n in range(2 * KC * 2 * 2 // 2):
                i0, c = 4 * (n // KC), n % KC
                bank = rot(n)
                for s in range(4):
                    last = nc.tensor.transpose(bank[:, P * s:P * s + P], yacc[:, i0 + s, P * c:P * c + P], ident[:, :])
                last.then_inc(rot_done, 1)
            for i in range(NT):
                pe.wait_ge(rot_free, 2 * (i // 4) + 2)
                for c in range(KC):
                    last = mm(ps[:, 2, E * i:E * i + E], x1T[:, c, P * i:P * i + P], gwT[:, c, :], start=c == 0, stop=c == KC - 1)
            last.then_inc(logit_done, 1)
            def shared_up(n):
                tc, (f0, fn) = n // 3, SFC[n % 3]
                if n >= 2:
                    pe.wait_ge(act_done, n - 1)
                for u in range(2):
                    for k in range(KC):
                        last = mm(ps[0:fn, 4 + 2 * (n % 2) + u, :], wsgu[:, k, SI * u + f0:SI * u + f0 + fn],
                                  x1T[:, k, 512 * tc:512 * tc + 512], start=k == 0, stop=k == KC - 1)
                last.then_inc(gu_done, 1)

            for n in range(SHARED_FIRST):
                shared_up(n)
            pe.wait_ge(sel_done, 1)
            for i in range(NT):
                last = mm(ps[:, 3, E * i:E * i + E], tri[:, :], sel[:, i, :], start=True, stop=i == 0)
                if i:
                    last = mm(ps[:, 3, E * i:E * i + E], onesb[:, :], selcum[:, i - 1, :], start=False, stop=True)
            last.then_inc(pos_done, 1)
            for n in range(SHARED_FIRST, SHARED_UNITS):
                shared_up(n)
            n = 8
            pe.wait_ge(onehot_done, 1)
            for q in range(3):
                bank = rot(n)
                for s in range(4):
                    m = 4 * q + s
                    for i in range(NT):
                        last = mm(bank[:, NI * s:NI * s + NI], onehot[:, i, P * m:P * m + P], info[:, i, :], start=i == 0, stop=i == NT - 1)
                last.then_inc(rot_done, 1)
                n += 1
            for q in range(3):
                pe.wait_ge(xg_in[q], 16 * 4)
                for c in range(KC):
                    bank = rot(n)
                    for s in range(4):
                        last = nc.tensor.transpose(bank[:, P * s:P * s + P], xg[:, 4 * q + s, P * c:P * c + P], ident[:, :])
                    last.then_inc(rot_done, 1)
                    n += 1
            pe.wait_ge(rot_free, n)
            pe.wait_ge(act_done, 12)
            with pe.Fori(0, E // EB) as g:
                def expert_down(k):
                    pe.wait_ge(eact_done, g * EB + k + 2)
                    pe.wait_ge(ey_evac, g * EB + max(k - 1, 0) + 1)
                    for u in range(2):
                        last = mm(ps[0:C, 6 + k % 2, 0:D], actE[0:FH, k % 4, u, :], wd[:, k, u, :], start=u == 0, stop=u == 1)
                    last.then_inc(ey_done, 1)

                for k in range(EB):
                    pe.wait_ge(ew_in[k], g * 32 + 32)
                    pe.wait_ge(eact_done, g * EB + max(k - 1, 0) + 1)
                    for f in range(4):
                        for c in range(KC):
                            last = mm(ps[0:FH, 4 + k % 2, C * f:C * f + C], wgu[:, k, c, FH * f:FH * f + FH],
                                      xbT[:, c, bass.ds(g * (EB * C) + k * C, C)], start=c == 0, stop=c == KC - 1)
                    last.then_inc(egu_done, 1)
                    if k:
                        expert_down(k - 1)
                expert_down(EB - 1)
            pe.wait_ge(yw_done, 1)
            for i in range(NT):
                if i >= 2:
                    pe.wait_ge(comb_free, i - 1)
                bank = ps[:, 2 + i % 2, 0:D]
                for c, (f0, fn) in enumerate(SFC):
                    mm(bank, actS[0:fn, c, P * i:P * i + P], wsd[0:fn, c, :], start=c == 0, stop=False)
                pe.wait_ge(oht_done, i + 1)
                for m in range(SC):
                    last = mm(bank, ohT[i % 2][:, m, :], ybuf[:, m, :], start=False, stop=m == SC - 1)
                last.then_inc(comb_done, 1)

        @block.scalar
        def _(act):
            for first in (tanh_done, ey_evac, *yb_in):
                act.sem_inc(first, 1)
            with act.Fori(0, H) as h:
                def square(b, m):
                    act.wait_ge(pj_free, h * UNITS + PROJ[b] + 2 * (m + 1) + 1)
                    if b == 1:
                        act.wait_ge(pj_done, h * UNITS + SSQ[0] + 1)
                    nc.scalar.activation((qsq, ksq)[m], (qraw, kT)[m][b], ACT.Square).then_inc(sq_done, 1)

                def tanh(b, j):
                    act.wait_ge(s_ready, h * (B * TT) + b * TT + j + 1)
                    act.wait_ge(r_done, h * B + b + 1)
                    buf = ps[:, 2 * (j % 2):2 * (j % 2) + 2, :].rearrange("p k n -> p (k n)")
                    nc.scalar.activation(probs[b][:, POFF[j]:POFF[j] + T - P * j], buf[:, P * j:T], ACT.Tanh,
                                         scale=rstd[b][:, TT + j:TT + j + 1]).then_inc(tanh_done, 1)

                def exp(b, j):
                    act.wait_ge(tanh_done, h * (B * TT) + b * TT + j + 2)
                    pj = probs[b][:, POFF[j]:POFF[j] + T - P * j]
                    nc.scalar.activation(pj, pj, ACT.Exp, scale=CAP).then_inc(exp_done, 1)

                for b in range(B):
                    square(b, 0)
                    square(b, 1)
                for b in range(B):
                    for j in range(TT):
                        tanh(b, j)
                        if j:
                            exp(b, j - 1)
                    exp(b, TT - 1)

            def shared_silu(n):
                fn = SFC[n % 3][1]
                act.wait_ge(gu_done, n + 1)
                if n >= 2:
                    act.wait_ge(act_done, n - 1)
                nc.scalar.activation(sil[n % 2][0:fn, :], ps[0:fn, 4 + 2 * (n % 2), :], ACT.Silu).then_inc(sil_done, 1)

            for n in range(4):
                shared_silu(n)
            act.wait_ge(diff_done, 1)
            nc.scalar.activation(wts[:, :, :], wts[:, :, :], ACT.Exp).then_inc(e_done, 1)
            for n in range(4, SHARED_UNITS):
                shared_silu(n)
            with act.Fori(0, E // EB) as g:
                for k in range(EB):
                    act.wait_ge(egu_done, g * EB + k + 1)
                    nc.scalar.activation(silE[0:FH, k % 4].rearrange("p k c -> p (k c)"), ps[0:FH, 4 + k % 2, 0:2 * C],
                                         ACT.Silu).then_inc(esil_done, 1)
                    act.wait_ge(ey_done, g * EB + k + 1)
                    act.wait_ge(yb_in[k % 4], g * YB_TURN[k % 4] + YB_BEFORE[k] + 1)
                    nc.scalar.activation(ye[0:C, k % 4, :], ps[0:C, 6 + k % 2, 0:D], ACT.Copy).then_inc(ey_evac, 1)
                    act.wait_ge(ey_evac, g * EB + k + 2)
                    for r0, p0, ch, rows in expert_pieces(k):
                        act.dma_start(ybuf[p0:p0 + rows, bass.ds(g * ECH + ch, 1), :].rearrange("p o d -> p (o d)"),
                                      ye[r0:r0 + rows, k % 4, :]).then_inc(yb_in[k % 4], 16)
            for i in range(NT):
                act.wait_ge(norm_done, 2 + i)
                act.dma_start(out_v[:, i, :], yacc[:, i, :]).then_inc(out_done, 16)

        @block.gpsimd
        def _(pool):
            nc.gpsimd.memset(ones[:, :], 1.0).then_inc(consts, 1)
            nc.gpsimd.memset(mhalf[:, :], -0.5).then_inc(consts, 1)
            nc.gpsimd.memset(causal[:, :], 1.0).then_inc(consts, 1)
            pool.wait_ge(consts, 3)
            nc.gpsimd.affine_select(out=causal[:, :], in_=causal[:, :], compare_op=ALU.is_ge, fill=0.0, base=0,
                                    pattern=[[1, P]], channel_multiplier=-1).then_inc(consts, 1)
            pool.wait_ge(consts, 4)
            pool.wait_ge(g_done, 5)
            with pool.Fori(0, H) as h:
                pool.wait_ge(qhat_done, h * B + 1)
                nc.gpsimd.tensor_copy(gcur, ghead[:, bass.ds(h, 1)]).then_inc(gcur_done, 1)
                for b in range(B):
                    pool.wait_ge(pj_free, h * UNITS + SSQ[b] + 2)
                    nc.gpsimd.tensor_tensor(rstd[b], var[b], mhalf[:, :], ALU.pow).then_inc(r_done, 1)
                for b in range(B):
                    for j in range(TT):
                        pool.wait_ge(exp_done, h * (B * TT) + b * TT + j + 1)
                        diag = probs[b][:, POFF[j]:POFF[j] + P]
                        nc.gpsimd.tensor_tensor(diag, diag, causal[:, :], ALU.mult).then_inc(mask_done, 1)
            nc.gpsimd.memset(ident[:, :], 0.0).then_inc(consts, 1)
            nc.gpsimd.memset(tri[:, :], 1.0).then_inc(consts, 1)
            nc.gpsimd.memset(onesb[:, :], 1.0).then_inc(consts, 1)
            nc.gpsimd.memset(emask[:, :, :], 1.0).then_inc(consts, 1)
            nc.gpsimd.iota(iota48[:, :], pattern=[[1, C]], base=0, channel_multiplier=0,
                           allow_small_or_imprecise_dtypes=True).then_inc(consts, 1)
            nc.gpsimd.iota(iota128[:, :], pattern=[[1, P]], base=0, channel_multiplier=0,
                           allow_small_or_imprecise_dtypes=True).then_inc(consts, 1)
            nc.gpsimd.iota(info[:, :, 3 * E:3 * E + 1], pattern=[[0, NT], [0, 1]], base=0, channel_multiplier=1,
                           allow_small_or_imprecise_dtypes=True).then_inc(consts, 1)
            nc.gpsimd.iota(info[:, :, 3 * E + 1:3 * E + 2], pattern=[[1, NT], [0, 1]], base=0, channel_multiplier=0,
                           allow_small_or_imprecise_dtypes=True).then_inc(consts, 1)
            nc.gpsimd.memset(info[:, :, 3 * E + 2:3 * E + 4], 1.0).then_inc(consts, 1)
            pool.wait_ge(consts, 13)
            nc.gpsimd.affine_select(out=ident[:, :], in_=ident[:, :], compare_op=ALU.not_equal, fill=1.0, base=0,
                                    pattern=[[1, P]], channel_multiplier=-1).then_inc(consts, 1)
            nc.gpsimd.affine_select(out=tri[:, :], in_=tri[:, :], compare_op=ALU.is_gt, fill=0.0, base=0,
                                    pattern=[[1, P]], channel_multiplier=-1).then_inc(consts, 1)
            nc.gpsimd.affine_select(out=emask[:, :, :], in_=emask[:, :, :], compare_op=ALU.is_ge, fill=0.0, base=0,
                                    pattern=[[P, SC], [-C, E]], channel_multiplier=1).then_inc(consts, 1)
            pool.wait_ge(consts, 16)
            nc.gpsimd.affine_select(out=emask[:, :, :], in_=emask[:, :, :], compare_op=ALU.is_gt, fill=0.0, base=C,
                                    pattern=[[-P, SC], [C, E]], channel_multiplier=-1).then_inc(consts, 1)
            pool.wait_ge(var1, 1)
            nc.gpsimd.tensor_tensor(lnr[:, :], lnv[:, :], mhalf[:, 0:NT], ALU.pow).then_inc(rln1, 1)
            pool.wait_ge(tok_done, 1)
            pool.wait_ge(x1_out, 16)
            for m in range(SC):
                nc.gpsimd.indirect_dma_start(xg[:, m, :], None, x1_d, bass.IndirectOffsetOnAxis(ap=toki[:, m:m + 1], axis=0)).then_inc(xg_in[m // 4], 16)
            for i in range(NT):
                pool.wait_ge(var2, i + 1)
                nc.gpsimd.tensor_tensor(lnr[:, i:i + 1], lnv[:, i:i + 1], mhalf[:, 0:1], ALU.pow).then_inc(rln2, 1)

        @block.vector
        def _(dve):
            v = nc.vector
            for first in (pj_free, o_evac, qhat_done, eact_done):
                dve.sem_inc(first, 1)
            dve.wait_ge(small_in, 64)
            v.tensor_tensor(gtmp[:, 2, :], gtmp[:, 0, :], gtmp[:, 0, :], ALU.mult).then_inc(g_done, 1)
            v.tensor_tensor(gtmp[:, 3, :], gtmp[:, 1, :], gtmp[:, 1, :], ALU.mult).then_inc(g_done, 1)
            v.tensor_tensor(nrm[:, 2, :], nrm[:, 0, :], nrm[:, 1, :], ALU.mult).then_inc(g_done, 1)
            dve.wait_ge(g_done, 3)
            v.tensor_tensor(gtmp[:, 2, :], gtmp[:, 2, :], gtmp[:, 3, :], ALU.add).then_inc(g_done, 1)
            dve.wait_ge(g_done, 4)
            v.tensor_scalar(ghead, gtmp[:, 2, :], nrm[:, 2, :], DH ** -0.5 / CAP, ALU.mult, ALU.mult).then_inc(g_done, 1)
            dve.wait_ge(x_in, 16)
            with dve.Fori(0, H) as h:
                def unit(k):
                    dve.wait_ge(pj_done, h * UNITS + k + 1)
                    return ps[:, PJ + k % 2, :]

                def projected(b):
                    k = PROJ[b]
                    for dst in (qraw[b], kT[b], vS[b].rearrange("p j d -> p (j d)")):
                        for half in range(2):
                            bank = unit(k)
                            v.tensor_copy(dst[:, 512 * half:512 * half + 512], bank).then_inc(pj_free, 1)
                            k += 1

                def mean_square(b):
                    bank = unit(SSQ[b])
                    v.tensor_scalar(var[b], bank[:, 0:2 * TT], 1.0 / DH, RMS_EPS, ALU.mult, ALU.add).then_inc(pj_free, 1)

                def scale_queries(b):
                    dve.wait_ge(rqB_in, h * (16 * B) + 16 * (b + 1))
                    dve.wait_ge(gcur_done, h + 1)
                    v.scalar_tensor_tensor(qhat[b], qraw[b], gcur, rqB[b], ALU.mult, ALU.mult).then_inc(qhat_done, 1)

                def add_probs(b, j):
                    dve.wait_ge(mask_done, h * (B * TT) + b * TT + j + 1)
                    pj = probs[b][:, POFF[j]:POFF[j] + T - P * j]
                    if j == 0:
                        v.tensor_copy(pacc[b], pj).then_inc(pacc_done, 1)
                    else:
                        dve.wait_ge(pacc_done, h * (B * TT) + b * TT + j)
                        v.tensor_tensor(pacc[b][:, P * j:T], pacc[b][:, P * j:T], pj, ALU.add).then_inc(pacc_done, 1)

                def take_output(b):
                    dve.wait_ge(o_ready, h * B + b + 1)
                    v.tensor_copy(oT[b], ps[:, 4:6, :].rearrange("p k n -> p (k n)")).then_inc(o_evac, 1)

                def finish(b):
                    bank = unit(SUMS[b])
                    v.reciprocal(rsum[b], bank[:, 0:TT]).then_inc(pj_free, 1)
                    dve.wait_ge(pj_free, h * UNITS + SUMS[b] + 2)
                    for u in range(4):
                        bank = unit(OUTP[b] + u)
                        for s in range(2):
                            i = 2 * u + s
                            y = yacc[:, b * TT + i, :]
                            last = v.scalar_tensor_tensor(y, bank[:, D * s:D * s + D], rsum[b][:, i:i + 1], y, ALU.mult, ALU.add)
                        last.then_inc(pj_free, 1)

                projected(0)
                mean_square(0)
                projected(1)
                scale_queries(0)
                mean_square(1)
                for j in range(TT):
                    add_probs(0, j)
                    if j == 3:
                        scale_queries(1)
                take_output(0)
                add_probs(1, 0)
                add_probs(1, 1)
                finish(0)
                for j in range(2, TT):
                    add_probs(1, j)
                take_output(1)
                finish(1)

            steps = [0]

            def step(ins):
                steps[0] += 1
                ins.then_inc(dstep, 1)

            def settle():
                dve.wait_ge(dstep, steps[0])

            dve.wait_ge(pj_free, H * UNITS + 1)
            for i in range(NT):
                step(v.bn_stats(stats[:, i, :], yacc[:, i, :]))
            settle()
            for i in range(NT):
                step(v.bn_aggr(mv[:, i, :], stats[:, i, :]))
            settle()
            v.tensor_scalar(lnv[:, :], mv[:, :, 1], LN_EPS, None, ALU.add).then_inc(var1, 1)
            dve.wait_ge(rln1, 1)
            for i in range(NT):
                ins = v.tensor_scalar(yacc[:, i, :], yacc[:, i, :], mv[:, i, 0:1], lnr[:, i:i + 1], ALU.subtract, ALU.mult)
            ins.then_inc(norm_done, 1)
            n = 0
            for n in range(8):
                i0, c = 4 * (n // KC), n % KC
                dve.wait_ge(rot_done, n + 1)
                v.tensor_copy(x1T[:, c, P * i0:P * i0 + 512], ps[:, n % 2, :]).then_inc(rot_free, 1)
            def shared_act(n):
                c, fn = n % 3, SFC[n % 3][1]
                tc = n // 3
                dve.wait_ge(sil_done, n + 1)
                v.tensor_tensor(actS[0:fn, c, 512 * tc:512 * tc + 512], sil[n % 2][0:fn, :],
                                ps[0:fn, 5 + 2 * (n % 2), :], ALU.mult).then_inc(act_done, 1)

            dve.wait_ge(consts, 17)
            dve.wait_ge(logit_done, 1)
            step(v.tensor_copy(lg[:, :, :].rearrange("p i e -> p (i e)"), ps[:, 2, :]))
            step(v.memset(grp[:, :, G:G + 5], NEG))
            step(v.memset(mk[:, :, E:E + 2], NEG))
            settle()
            step(v.tensor_reduce(grp[:, :, 0:G], lg[:, :, :].rearrange("p i (g e) -> p i g e", e=EG), AX, ALU.max))
            settle()
            for i in range(NT):
                step(v.max(t8[:, i, :], grp[:, i, 0:G]))
            shared_act(0)
            settle()
            step(v.memset(t8[:, :, TOPG:8], NEG))
            settle()
            for i in range(NT):
                step(v.match_replace(grep[:, i, :], t8[:, i, :], grp[:, i, :], POS))
            shared_act(1)
            settle()
            step(v.tensor_tensor(keep[:, :, :], grep[:, :, 0:G], grp[:, :, 0:G], ALU.not_equal))
            settle()
            step(v.tensor_tensor(lg[:, :, :].rearrange("p i (g e) -> p (i g) e", e=EG),
                                 lg[:, :, :].rearrange("p i (g e) -> p (i g) e", e=EG),
                                 keep[:, :, :].rearrange("p i g -> p (i g)").unsqueeze(2).to_broadcast([P, NT * G, EG]), ALU.mult))
            settle()
            step(v.tensor_scalar(mk[:, :, 0:E], lg[:, :, :], 0.0, None, ALU.add))
            settle()
            shared_act(2)
            for i in range(NT):
                step(v.max(m8[:, i, :], mk[:, i, 0:E]))
            settle()
            v.tensor_tensor(wts[:, :, :], mk[:, :, 0:E], m8[:, :, 0:1].to_broadcast([P, NT, E]), ALU.subtract).then_inc(diff_done, 1)
            shared_act(3)
            dve.wait_ge(diff_done, 1)
            step(v.memset(m8[:, :, TOPK:8], NEG))
            settle()
            for i in range(NT):
                step(v.match_replace(mrep[:, i, :], m8[:, i, :], mk[:, i, :], POS))
            settle()
            v.tensor_tensor(sel[:, :, :], mrep[:, :, 0:E], mk[:, :, 0:E], ALU.not_equal).then_inc(dstep, 1)
            steps[0] += 1
            settle()
            step(v.tensor_copy(selcum[:, 0, :], sel[:, 0, :]))
            for i in range(1, NT - 1):
                settle()
                step(v.tensor_tensor(selcum[:, i, :], selcum[:, i - 1, :], sel[:, i, :], ALU.add))
            settle()
            v.memset(zero[:, :], 0.0).then_inc(sel_done, 1)
            shared_act(4)
            shared_act(5)
            dve.wait_ge(e_done, 1)
            step(v.tensor_reduce(srow[:, :], wts[:, :, :], AX, ALU.add))
            settle()
            step(v.reciprocal(rrow[:, :], srow[:, :]))
            settle()
            step(v.tensor_scalar(rrow[:, :], rrow[:, :], ROUTE_SCALE, None, ALU.mult))
            settle()
            step(v.tensor_tensor(wts[:, :, :], wts[:, :, :], rrow[:, :].unsqueeze(2).to_broadcast([P, NT, E]), ALU.mult))
            settle()
            step(v.tensor_copy(info[:, :, 0:E], wts[:, :, :]))
            settle()
            step(v.tensor_tensor(wrest[:, :, :], wts[:, :, :], info[:, :, 0:E], ALU.subtract))
            settle()
            step(v.tensor_copy(info[:, :, E:2 * E], wrest[:, :, :]))
            settle()
            step(v.tensor_tensor(wrest[:, :, :], wrest[:, :, :], info[:, :, E:2 * E], ALU.subtract))
            settle()
            step(v.tensor_copy(info[:, :, 2 * E:3 * E], wrest[:, :, :]))
            step(v.tensor_scalar(posm[:, :, :], sel[:, :, :], -4096.0, 4096.0, ALU.mult, ALU.add))
            settle()
            dve.wait_ge(pos_done, 1)
            step(v.tensor_tensor(posm[:, :, :].rearrange("p i e -> p (i e)"), posm[:, :, :].rearrange("p i e -> p (i e)"), ps[:, 3, :], ALU.add))
            settle()

            for i in range(NT):
                ins = v.tensor_tensor(onehot[:, i, :].rearrange("p (e c) -> p e c", c=C),
                                      posm[:, i, :].unsqueeze(2).to_broadcast([P, E, C]),
                                      iota48[:, :].unsqueeze(1).to_broadcast([P, E, C]), ALU.is_equal)
                if i == NT - 1:
                    ins.then_inc(onehot_done, 1)
                if i % 2 and 6 + i // 2 < SHARED_UNITS:
                    shared_act(6 + i // 2)
            for q in range(3):
                dve.wait_ge(rot_done, 8 + q + 1)
                v.tensor_copy(slot[:, 4 * q:4 * q + 4, :].rearrange("p m n -> p (m n)"), ps[:, (8 + q) % 2, 0:4 * NI]).then_inc(rot_free, 1)
            dve.wait_ge(rot_free, 11)
            step(v.scalar_tensor_tensor(tokr[:, 0, :], slot[:, :, 3 * E + 1], float(P), slot[:, :, 3 * E], ALU.mult, ALU.add))
            settle()
            step(v.tensor_tensor(tokr[:, 1, :], tokr[:, 0, :], slot[:, :, 3 * E + 2], ALU.add))
            v.tensor_copy(toki[:, :], tokr[:, 0, :]).then_inc(tok_done, 1)
            settle()
            step(v.tensor_scalar(tok[:, :], tokr[:, 1, :], -1.0, None, ALU.add))
            for part_ in range(3):
                dst = wsl if part_ == 0 else wsl
                if part_ == 0:
                    step(v.tensor_tensor(wsl[:, :, :], slot[:, :, 0:E], slot[:, :, E:2 * E], ALU.add))
                elif part_ == 1:
                    step(v.tensor_tensor(wsl[:, :, :], wsl[:, :, :], slot[:, :, 2 * E:3 * E], ALU.add))
                else:
                    step(v.tensor_tensor(wsl[:, :, :], wsl[:, :, :], emask[:, :, :], ALU.mult))
                settle()
            step(v.tensor_reduce(wslot[:, :], wsl[:, :, :], AX, ALU.add))
            settle()
            for n in range(6):
                q, c = n // KC, n % KC
                dve.wait_ge(rot_done, 11 + n + 1)
                v.tensor_copy(xbT[:, c, 512 * q:512 * q + 512], ps[:, (11 + n) % 2, :]).then_inc(rot_free, 1)
            with dve.Fori(0, E // EB) as g:
                for k in range(EB):
                    dve.wait_ge(esil_done, g * EB + k + 1)
                    v.tensor_tensor(actE[0:FH, k % 4].rearrange("p k c -> p (k c)"), silE[0:FH, k % 4].rearrange("p k c -> p (k c)"),
                                    ps[0:FH, 4 + k % 2, 2 * C:4 * C], ALU.mult).then_inc(eact_done, 1)
            for s in range(4):
                dve.wait_ge(yb_in[s], YB_TURN[s] * (E // EB) + 1)
            for m in range(SC):
                ins = v.tensor_scalar(ybuf[:, m, :], ybuf[:, m, :], wslot[:, m:m + 1], None, ALU.mult)
            ins.then_inc(yw_done, 1)

            def back_to_tokens(i):
                if i >= 2:
                    dve.wait_ge(comb_done, i - 1)
                step(v.tensor_scalar(tokc[:, i, :], tok[:, :], -float(P * i), None, ALU.add))
                settle()
                v.tensor_tensor(ohT[i % 2], tokc[:, i, :].unsqueeze(2).to_broadcast([P, SC, P]),
                                iota128[:, :].unsqueeze(1).to_broadcast([P, SC, P]), ALU.is_equal).then_inc(oht_done, 1)

            back_to_tokens(0)
            for i in range(NT):
                if i + 1 < NT:
                    back_to_tokens(i + 1)
                dve.wait_ge(comb_done, i + 1)
                v.tensor_tensor(yacc[:, i, :], yacc[:, i, :], ps[:, 2 + i % 2, 0:D], ALU.add).then_inc(comb_free, 1)
                dve.wait_ge(comb_free, i + 1)
                step(v.bn_stats(stats[:, i, :], yacc[:, i, :]))
                settle()
                step(v.bn_aggr(mv[:, i, :], stats[:, i, :]))
                settle()
                v.tensor_scalar(lnv[:, i:i + 1], mv[:, i, 1:2], LN_EPS, None, ALU.add).then_inc(var2, 1)
                if i:
                    dve.wait_ge(rln2, i)
                    v.tensor_scalar(yacc[:, i - 1, :], yacc[:, i - 1, :], mv[:, i - 1, 0:1], lnr[:, i - 1:i], ALU.subtract, ALU.mult).then_inc(norm_done, 1)
            dve.wait_ge(rln2, NT)
            v.tensor_scalar(yacc[:, NT - 1, :], yacc[:, NT - 1, :], mv[:, NT - 1, 0:1], lnr[:, NT - 1:NT], ALU.subtract, ALU.mult).then_inc(norm_done, 1)


def _yb_counts():
    turn, at_ = [0] * 4, []
    for k in range(EB):
        pieces = 1 + ((k * C) // P != ((k + 1) * C - 1) // P)
        at_.append(turn[k % 4])
        turn[k % 4] += 16 * pieces
    return turn, at_


YB_TURN, YB_BEFORE = _yb_counts()


def kernel(**inputs):
    import concourse.bacc as bacc
    from concourse.bass_utils import run_bass_kernel_spmd as run

    a = {n: np.asarray(v) for n, v in inputs.items()}
    x = a["L0_attn_x"].reshape(N, D)

    def heads(w):
        return w.reshape(H, DH, KC, P).transpose(0, 3, 2, 1)

    wqkv = np.stack([heads(a["L0_attn_wq"]), heads(a["L0_attn_wk"]), heads(a["L0_attn_wv"])], axis=2)
    wo = a["L0_attn_wo"].reshape(D, H, DH).transpose(1, 2, 0)

    def rope(t):
        return np.repeat(t[:H], 2, axis=1).T

    arrays = {
        "x": x, "xT": x.T, "wqkv": wqkv, "wo": wo,
        "qn": a["L0_attn_q_norm_w"].reshape(DH, 1), "kn": a["L0_attn_k_norm_w"].reshape(DH, 1),
        "cos": rope(a["L0_attn_rope_cos"]), "sin": rope(a["L0_attn_rope_sin"]),
        "gw": a["L0_ffn_gate_w"].T, "wgu": a["L0_ffn_w_gate_up"], "wd": a["L0_ffn_w_down"],
        "wsgu": a["L0_ffn_ws_gate_up"], "wsd": a["L0_ffn_ws_down"],
    }
    nc = bacc.Bacc("TRN2", target_bir_lowering=False, num_devices=1)
    feed, args = {}, []
    for name, arr in arrays.items():
        arr = np.ascontiguousarray(arr)
        feed[f"in_{name}"] = arr
        args.append(nc.dram_tensor(f"in_{name}", arr.shape, mybir.dt.from_np(arr.dtype), kind="ExternalInput").ap())
    args.append(nc.dram_tensor("out_0", (N, D), F32, kind="ExternalOutput").ap())
    block_kernel(nc, *args)
    r = run(nc, [feed], core_ids=[0])
    return r.results[0]["out_0"].reshape(B, T, D)
```

```python
import numpy as np
import concourse.bass as bass
from concourse import mybir
from concourse.alu_op_type import AluOpType as ALU
from contextlib import ExitStack

F32 = mybir.dt.float32
F32R = mybir.dt.float32r
BF16 = mybir.dt.bfloat16
I32 = mybir.dt.int32
ACT = mybir.ActivationFunctionType
AX = mybir.AxisListType.X

P = 128
B, T, D = 2, 1024, 256
H, DH = 16, 128
N = B * T
NT = N // P
TT = T // P
KC = D // P
CAP = 50.0
RMS_EPS, LN_EPS = 1e-6, 1e-5
E, G, TOPG, TOPK, C = 32, 8, 3, 6, 48
EG = E // G
FI = 176
FH = FI // 2
SI = 2 * FI
SFC = [(0, 128), (128, 128), (256, 96)]
ROUTE_SCALE = 16.0
SLOTS = E * C
SC = SLOTS // P
EB = 8
ECH = EB * C // P
TURNS = E // EB
NEG = -3.0e38
POS = 3.0e38
NI = 3 * E + 4
PAD = NT // 2
HELPED = (6, 8, 10, 12, 14, 15)
SR = 2

RING = 4
PJ = 6

PROLOGUE = "q0 q1 k0 k1 ss v0 v1".split()
PE_STEP = """q0 S0 q1 k0 S1 k1 pv4' sums0 sums1 pv5' pv6' S2 ss0 pv7' ss1 S3 S4 ss2 ss3 S5 op0 op1 pv0 v0 op2
             pv1 S6 op3 pv2 pv3 S7 v1""".split()
ACT_STEP = """t0 h6' e7' q k0 h7' e0 t1 k1 e1 h0 t2 O e2 t3 h1 t4 e3 h2 h3 v0 t5 e4 e5 t6 e6 h4 h5 t7 v1""".split()
DVE_STEP = """q0 q1 l5' k0 wqk l6' k1 l7' sums l0 O wo ss l1 op0 l2 op1 v0 l3 op2 op3 qf l4 v1""".split()
POOL_STEP = """g m7' m0 m1 m2 ss m3 m4 m5 m6""".split()
AHEAD = {"q0", "q1", "q", "k0", "k1", "v0", "v1", "ss", "ss0", "ss1", "ss2", "ss3", "qf", "wqk", "g"}
BEHIND = {"sums", "sums0", "sums1", "O", "op0", "op1", "op2", "op3"}
PARTS = {"sums0": "sums", "sums1": "sums", "ss0": "ss", "ss1": "ss", "ss2": "ss", "ss3": "ss"}
INNER = {"sums0", "ss0", "ss1", "ss2"}
NOT_UNITS = INNER | {"q", "qf", "wqk", "g", "O"}


def work(step, first=False, last=False):
    return [k for k in step if not (first and (k in BEHIND or k.endswith("'"))) and not (last and k in AHEAD)]


def tail(step, *more):
    return [k for k in step if k.endswith("'")] + list(more)


TAIL = {"pe": tail(PE_STEP, "sums0", "sums1", "op0", "op1", "op2", "op3"), "act": tail(ACT_STEP, "O"),
        "dve": tail(DVE_STEP, "O", "sums", "op0", "op1", "op2", "op3"), "pool": tail(POOL_STEP)}


def units(steps):
    return [(b, PARTS.get(k, k)) for b, step in enumerate(steps) for k in step if k in (AHEAD | BEHIND) - NOT_UNITS]


UNITS_FIRST = units([work(PE_STEP, first=True), work(PE_STEP)])
UNITS_HEAD = units([work(PE_STEP), work(PE_STEP)])
UNITS_LAST = units([work(PE_STEP), work(PE_STEP, last=True)])
UNITS_TAIL = units([TAIL["pe"]])
BASE1 = len(PROLOGUE) + len(UNITS_FIRST)
BASE_TAIL = BASE1 + (H - 2) * len(UNITS_HEAD) + len(UNITS_LAST)
UNITS_ALL = BASE_TAIL + len(UNITS_TAIL)


class Head:

    def __init__(self, h, kind):
        self.h = h
        self.first, self.last = kind == "first", kind == "last"
        self.units = {"first": UNITS_FIRST, "middle": UNITS_HEAD, "last": UNITS_LAST, "tail": UNITS_TAIL}[kind]
        self.base = {"first": len(PROLOGUE), "tail": BASE_TAIL}.get(kind, (h - 1) * len(UNITS_HEAD) + BASE1)
        self.parity = {"first": len(PROLOGUE), "tail": BASE_TAIL}.get(kind, BASE1) % 2

    def steps(self, step):
        return [(0, work(step, first=self.first)), (1, work(step, last=self.last))]

    def unit(self, b, k):
        n = self.units.index((b, k))
        return self.base + n + 1, PJ + (self.parity + n) % 2


CONSTS = 15

SHARED_UNITS = N // 512 * len(SFC)
SHARED_FIRST = 4
SHARED_SECOND = 10


def block_kernel(nc, x, xT_d, wqkv_d, wo_d, qn, kn, cos_d, sin_d, gw_d, wgu_d, wd_d, wsgu_d, wsd_d, out):
    rq_d = nc.dram_tensor("rq_rows", (B, T), F32, kind="Internal").ap()
    x1_d = nc.dram_tensor("x1_rows", (N, D), F32, kind="Internal").ap()

    ctx = ExitStack()
    with ctx:
        def sb(name, shape, dt=F32):
            return ctx.enter_context(nc.sbuf_tensor(name, shape, dt))

        def sem(name):
            return ctx.enter_context(nc.semaphore(name))

        yacc = sb("yacc", [P, NT, D])
        ones = sb("ones", [P, 2])
        causal = sb("causal", [P, P])
        mhalf = sb("mhalf", [P, 2 * TT])

        ident = sb("ident", [P, P])
        tri = sb("tri", [P, P], BF16)
        onesb = sb("onesb", [P, P], BF16)
        iota48 = sb("iota48", [P, C], BF16)
        slotsel = sb("slotsel", [P, 3])
        gwT = sb("gwT", [P, KC, E])
        stats = sb("stats", [P, NT, 6])
        mv = sb("mv", [P, NT, 2])
        lnv = sb("lnv", [P, NT])
        lnr = sb("lnr", [P, NT])

        att = ExitStack()

        def asb(name, shape, dt=F32):
            return att.enter_context(nc.sbuf_tensor(name, shape, dt))

        def pair(name, shape):
            return asb(name + "_hi", shape, F32R), asb(name + "_lo", shape, F32R)

        xT = pair("xT", [P, KC, N])
        xraw = asb("xraw", [P, KC, N])
        wraw = asb("wraw", [P, 2, KC, DH])
        wqk = pair("wqk", [P, 2, KC, DH])
        wv = asb("wv", [P, KC, DH])
        woraw = asb("woraw", [P, D])
        wo = pair("wo", [P, D])
        praw = asb("praw", [P, RING, T])
        prob = pair("prob", [P, RING, T])
        pacc = asb("pacc", [P, B, T])
        qraw = asb("qraw", [P, T])
        qhat = pair("qhat", [P, B, T])
        kT = pair("kT", [P, B, T])
        vS = pair("vS", [P, B, T])
        rqB = asb("rqB", [P, T])
        oT = pair("oT", [P, T])
        qsq = asb("qsq", [P, T])
        ksq = asb("ksq", [P, T])
        var = asb("var", [P, B, 2 * TT])
        rstd = asb("rstd", [P, B, 2 * TT])
        rsum = asb("rsum", [P, B, TT])
        ghead = asb("ghead", [P, H])
        gcur = asb("gcur", [P, 1])
        gtmp = asb("gtmp", [P, 4, H])
        nrm = asb("nrm", [P, 3, 1])
        att.close()

        wgu = sb("wgu", [P, EB, KC, 2 * FI])
        wd = sb("wd", [FH, EB, 2, D])
        iota128 = sb("iota128", [P, P])
        tokc = sb("tokc", [P, NT, SC])
        wslot = sb("wslot", [P, SC])
        xbT = sb("xbT", [P, KC, SLOTS])

        route = ExitStack()

        def rsb(name, shape, dt=F32):
            return route.enter_context(nc.sbuf_tensor(name, shape, dt))

        sdown = rsb("sdown", [P, 2, D])
        tile0 = rsb("tile0", [P, NT, SC])
        info = rsb("info", [P, NT, NI], BF16)
        emask = rsb("emask", [P, SLOTS])
        wsgu = rsb("wsgu", [P, KC, 2 * SI])
        wsd = rsb("wsd", [P, 3, D])
        x1T = rsb("x1T", [P, KC, N])
        actS = rsb("actS", [P, 3, N])
        silu_s = rsb("silu_s", [P, SR, 512])
        up_s = rsb("up_s", [P, SR, 512])
        lg = rsb("lg", [P, NT, E])
        mk = rsb("mk", [P, NT, E + 2])
        mrep = rsb("mrep", [P, NT, E + 2])
        wts = rsb("wts", [P, NT, E])
        grp = rsb("grp", [P, NT, G + 5])
        grep = rsb("grep", [P, NT, G + 5])
        keep = rsb("keep", [P, NT, G])
        m8 = rsb("m8", [P, NT, 8])
        g8 = rsb("g8", [P, NT, 8])
        srow = rsb("srow", [P, NT])
        rrow = rsb("rrow", [P, NT])
        sel = rsb("sel", [P, PAD + NT, E], BF16)
        cum = [rsb(f"cum{k}", [P, PAD + NT, E], BF16) for k in range(2)]
        posm = rsb("posm", [P, NT, E])
        posb = rsb("posb", [P, NT, E], BF16)
        wrest = rsb("wrest", [P, NT, E])
        tok = rsb("tok", [P, SC])
        toki = rsb("toki", [P, SC], I32)
        places = ExitStack()
        onehot = places.enter_context(nc.sbuf_tensor("onehot", [P, NT, SLOTS], BF16))
        places.close()
        minfo = rsb("minfo", [P, SLOTS])
        xg = rsb("xg", [P, SC, D])
        route.close()

        ohT = sb("ohT", [P, NT, SC, P], F32R)
        ybuf = sb("ybuf", [P, SC, D])
        y_hi = sb("y_hi", [P, SC, D], F32R)
        y_lo = sb("y_lo", [P, SC, D], F32R)
        ye = sb("ye", [P, 4, D])
        silE = sb("silE", [P, 2, 2 * C])
        actE = sb("actE", [P, 2, 2, C])

        ps = ctx.enter_context(nc.psum_tensor("ps", [P, 8, 512], F32))

        x_in = sem("x_in")
        xT_in = [sem(f"xT_in{b}") for b in range(B)]
        small_in, w_in, wv_in, wo_in = sem("small_in"), sem("w_in"), sem("wv_in"), sem("wo_in")
        consts, g_done, gcur_done = sem("consts"), sem("g_done"), sem("gcur_done")
        xhi_done, xlo_done = sem("xhi_done"), sem("xlo_done")
        whi_done, wlo_done = sem("whi_done"), sem("wlo_done")
        wohi_done, wolo_done = sem("wohi_done"), sem("wolo_done")
        pj_done, pj_free = sem("pj_done"), sem("pj_free")
        kvhi_done, sq_done = sem("kvhi_done"), sem("sq_done")
        r_done, rq_out, rqB_in = sem("r_done"), sem("rq_out"), sem("rqB_in")
        qf_done, qhi_done, qlo_done = sem("qf_done"), sem("qhi_done"), sem("qlo_done")
        s_ready, tanh_done, exp_done = sem("s_ready"), sem("tanh_done"), sem("exp_done")
        mask_done, phi_done, plo_done = sem("mask_done"), sem("phi_done"), sem("plo_done")
        pacc_done, pv_done = sem("pacc_done"), sem("pv_done")
        ohi_done, o_evac = sem("ohi_done"), sem("o_evac")
        wv_free = sem("wv_free")
        waited = sem("waited")
        dstep = sem("dstep")
        var1, rln1, x1_done = sem("var1"), sem("rln1"), sem("x1_done")
        moe_in, x1_out = sem("moe_in"), sem("x1_out")
        x1t_done, x1t_read, pads = sem("x1t_done"), sem("x1t_read"), sem("pads")
        logit_done = sem("logit_done")
        diff_done, e_done, sel_done = sem("diff_done"), sem("e_done"), sem("sel_done")
        pos_done, info_in, onehot_done = sem("pos_done"), sem("info_in"), sem("onehot_done")
        infot_done, minfo_done, slot_done, slot_read = sem("infot_done"), sem("minfo_done"), sem("slot_done"), sem("slot_read")
        gu_done, gu_read, act_done = sem("gu_done"), sem("gu_read"), sem("act_done")
        sd_done, sd_read, sd_added = sem("sd_done"), sem("sd_read"), sem("sd_added")
        apart_done, posb_done = sem("apart_done"), sem("posb_done")
        tok_done, tokc_done = sem("tok_done"), sem("tokc_done")
        xg_in = [sem(f"xg_in{q}") for q in range(3)]
        xbt_done, xbt_read = sem("xbt_done"), sem("xbt_read")
        ew_in = [sem(f"ew_in{k}") for k in range(EB)]
        egu_done, esil_done, eact_done = sem("egu_done"), sem("esil_done"), sem("eact_done")
        ey_done, ey_evac = sem("ey_done"), sem("ey_evac")
        yb_in = [sem(f"yb_in{k}") for k in range(4)]
        yw_done, yhi_done, ylo_done = sem("yw_done"), sem("yhi_done"), sem("ylo_done")
        oht_done, comb_done, comb_free = sem("oht_done"), sem("comb_done"), sem("comb_free")
        var2, rln2, norm_done, out_done = sem("var2"), sem("rln2"), sem("norm_done"), sem("out_done")

        block = ctx.enter_context(nc.Block())
        x_v = x.rearrange("(i p) d -> p i d", p=P)
        x1_v = x1_d.rearrange("(i p) d -> p i d", p=P)
        out_v = out.rearrange("(i p) d -> p i d", p=P)
        wgu_v = wgu_d.rearrange("e (c p) f -> e p c f", p=P)
        wd_v = wd_d.rearrange("e (c p) n -> e p c n", p=FH)

        def expert_pieces(k):
            lo, hi = k * C, (k + 1) * C
            out_, r = [], lo
            while r < hi:
                n = min(hi, (r // P + 1) * P) - r
                out_.append((r - lo, r % P, r // P, n))
                r += n
            return out_

        @block.sync
        def _(sp):
            sp.dma_start(wraw[:, :, :, :], wqkv_d[0, :, 0:2]).then_inc(w_in, 16)
            sp.dma_start(xraw[:, 0, 0:T], xT_d[0:P, 0:T]).then_inc(xT_in[0], 16)
            sp.dma_start(wv[:, :, :], wqkv_d[0, :, 2]).then_inc(wv_in, 16)
            for c in range(KC):
                sp.dma_start(xraw[:, c, T:N], xT_d[P * c:P * c + P, T:N]).then_inc(xT_in[1], 16)
            sp.dma_start(woraw[:, :], wo_d[0]).then_inc(wo_in, 16)
            sp.dma_start(gwT[:, :, :], gw_d.rearrange("(c p) e -> p c e", p=P)).then_inc(moe_in, 16)
            sp.dma_start(yacc[:, :, :], x_v).then_inc(x_in, 16)

            def rq_broadcast(step, b):
                sp.wait_ge(r_done, step + 1)
                sp.dma_start(rq_d[b].rearrange("(p j) -> p j", p=P), rstd[:, b, 0:TT]).then_inc(rq_out, 16)
                sp.wait_ge(rq_out, step * 16 + 16)
                sp.dma_start(rqB[:, :], rq_d[b:b + 1, :].to_broadcast([P, T])).then_inc(rqB_in, 16)

            rq_broadcast(0, 0)
            with sp.Fori(0, H - 1) as h:
                sp.wait_ge(wlo_done, h + 1)
                sp.dma_start(wraw[:, :, :, :], wqkv_d[bass.ds(h + 1, 1), :, 0:2].rearrange("o p m c d -> p (o m) c d")).then_inc(w_in, 16)
                rq_broadcast(h * B + 1, 1)
                sp.wait_ge(wv_free, h + 1)
                sp.dma_start(wv[:, :, :], wqkv_d[bass.ds(h + 1, 1), :, 2].rearrange("o p c d -> p (o c) d")).then_inc(wv_in, 16)
                sp.wait_ge(wolo_done, h + 1)
                sp.dma_start(woraw[:, :], wo_d[bass.ds(h + 1, 1)].rearrange("o p n -> p (o n)")).then_inc(wo_in, 16)
                rq_broadcast(h * B + 2, 0)
            rq_broadcast(H * B - 1, 1)

            sp.wait_ge(pj_free, UNITS_ALL)
            sp.dma_start(wsgu[:, :, :], wsgu_d.rearrange("(c p) f -> p c f", p=P)).then_inc(moe_in, 16)
            for c, (f0, fn) in enumerate(SFC):
                sp.dma_start(wsd[0:fn, c, :], wsd_d[f0:f0 + fn, :]).then_inc(moe_in, 16)
            for k in range(EB):
                if k % 4 == 2:
                    sp.wait_ge(x1_done, k // 4 + 1)
                    sp.dma_start(x1_v[:, TT * (k // 4):TT * (k // 4) + TT], yacc[:, TT * (k // 4):TT * (k // 4) + TT, :]).then_inc(x1_out, 16)
                sp.dma_start(wgu[:, k], wgu_v[k]).then_inc(ew_in[k], 16)
                sp.dma_start(wd[:, k], wd_v[k]).then_inc(ew_in[k], 16)
            with sp.Fori(0, TURNS - 1) as g:
                for k in range(EB):
                    sp.wait_ge(ey_done, g * EB + k + 1)
                    sp.dma_start(wgu[:, k], wgu_v[bass.ds(g * EB + (EB + k), 1)].rearrange("o p c f -> p (o c) f")).then_inc(ew_in[k], 16)
                    sp.dma_start(wd[:, k], wd_v[bass.ds(g * EB + (EB + k), 1)].rearrange("o p c n -> p (o c) n")).then_inc(ew_in[k], 16)
            sp.wait_ge(out_done, 16 * NT)

        @block.tensor
        def _(pe):
            mm = nc.tensor.matmul
            pe.sem_inc(pv_done, RING)

            def mm3(out_, left, right, start, stop):
                mm(out_, left[0], right[0], start=start, stop=False)
                mm(out_, left[0], right[1], start=False, stop=False)
                return mm(out_, left[1], right[0], start=False, stop=stop)

            def of(pair_, *at_):
                return tuple(t[at_] for t in pair_)

            ALL = slice(None)

            def open_unit(count):
                if not isinstance(count, int) or count > 2:
                    pe.wait_ge(pj_free, count - 2)

            def project(what, b, count, bank_no):
                open_unit(count)
                bank = ps[:, bank_no, :]
                half = int(what[1])
                if what[0] in "qk":
                    m, t0 = "qk".index(what[0]), b * T + 512 * half
                    for c in range(KC):
                        last = mm3(bank, of(wqk, ALL, m, c, ALL), of(xT, ALL, c, slice(t0, t0 + 512)), c == 0, c == KC - 1)
                else:
                    for j in range(4):
                        t0 = b * T + 512 * half + P * j
                        for c in range(KC):
                            last = mm(bank[:, P * j:P * j + P], xraw[:, c, t0:t0 + P], wv[:, c, :], start=c == 0, stop=c == KC - 1)
                last.then_inc(pj_done, 1)

            def sums_of_squares(step, part, count, bank_no):
                if part == 0:
                    open_unit(count)
                    pe.wait_ge(sq_done, step * 3 + 3)
                bank = ps[:, bank_no, :]
                for j in range(4 * part, 4 * part + 4):
                    if j < TT:
                        left = qsq[:, :].rearrange("d (p j) -> d j p", j=TT)[:, j, :]
                    else:
                        left = ksq[:, P * (j - TT):P * (j - TT) + P]
                    last = mm(bank[:, j:j + 1], left, ones[:, 0:1], start=True, stop=True)
                if part == 3:
                    last.then_inc(pj_done, 1)

            def scores(s, b, j):
                pe.wait_ge(tanh_done, s * TT + (1 if j == 0 else j))
                buf = ps[:, 2 * (j % 2):2 * (j % 2) + 2, :].rearrange("p k n -> p (k n)")
                for t0, t1 in ([(P * j, 512), (512, T)] if j < 4 else [(P * j, T)]):
                    last = mm3(buf[:, t0:t1], of(kT, ALL, b, slice(P * j, P * j + P)), of(qhat, ALL, b, slice(t0, t1)), True, True)
                last.then_inc(s_ready, 1)

            def values(s, b, j):
                if j == 0:
                    pe.wait_ge(o_evac, s + 1)
                pe.wait_ge(plo_done, s * TT + j + 1 + RING)
                o = ps[:, 4:6, :].rearrange("p k n -> p (k n)")
                for t0, t1 in ([(P * j, 512), (512, T)] if j < 4 else [(P * j, T)]):
                    last = mm3(o[:, t0:t1], of(vS, ALL, b, slice(P * j, P * j + P)), of(prob, ALL, j % RING, slice(t0 - P * j, t1 - P * j)),
                               j == 0, (j == 3 and t1 == 512) or j == TT - 1)
                last.then_inc(pv_done, 1)

            def sums(s, b, part, count, bank_no):
                if part == 0:
                    open_unit(count)
                    pe.wait_ge(pacc_done, (s + 1) * TT + RING)
                for j in range(4 * part, 4 * part + 4):
                    last = mm(ps[:, bank_no, j:j + 1], pacc[:, b, P * j:P * j + P], ones[:, 0:1], start=True, stop=True)
                if part == 1:
                    last.then_inc(pj_done, 1)

            def out_proj(s, b, u, count, bank_no):
                open_unit(count)
                if u == 0:
                    pe.wait_ge(o_evac, s + 2)
                for i in range(2):
                    t0 = P * (2 * u + i)
                    last = mm3(ps[:, bank_no, D * i:D * i + D], of(oT, ALL, slice(t0, t0 + P)), of(wo, ALL, ALL), True, True)
                last.then_inc(pj_done, 1)

            pe.wait_ge(consts, 4)
            pe.wait_ge(xlo_done, 1)
            pe.wait_ge(wlo_done, 1)
            for n, what in enumerate(PROLOGUE):
                if what == "ss":
                    for part in range(4):
                        sums_of_squares(0, part, n + 1, PJ + n % 2)
                else:
                    if what == "v0":
                        pe.wait_ge(wv_in, 16)
                    project(what, 0, n + 1, PJ + n % 2)
            pe.wait_ge(xlo_done, 2)

            def run(hd, steps, h):
                for b, step in steps:
                    s = h * B + b
                    for k in step:
                        if k == "S0":
                            pe.wait_ge(qlo_done, s + 1)
                        if k[0] == "S":
                            scores(s, b, int(k[1]))
                        elif k[:2] == "pv":
                            prev = k.endswith("'")
                            values(s - prev, (b + prev) % B, int(k[2]))
                        elif k[:4] == "sums":
                            sums(s - 1, 1 - b, int(k[4]), *hd.unit(b, "sums"))
                        elif k[:2] == "op":
                            if k == "op0" and b == 1:
                                pe.wait_ge(wolo_done, h + 1)
                            out_proj(s - 1, 1 - b, int(k[2]), *hd.unit(b, k))
                        elif k[:2] == "ss":
                            sums_of_squares(s + 1, int(k[2]), *hd.unit(b, "ss"))
                        else:
                            if k == "q0" and b == 1:
                                pe.wait_ge(wlo_done, h + 2)
                            if k == "v0" and b == 1:
                                pe.wait_ge(wv_in, (h + 2) * 16)
                            project(k, 1 - b, *hd.unit(b, k))

            def head(h, kind):
                hd = Head(h, kind)
                run(hd, hd.steps(PE_STEP), h)

            head(0, "first")
            with pe.Fori(1, H - 1) as h:
                head(h, "middle")
            head(H - 1, "last")
            run(Head(H, "tail"), [(0, TAIL["pe"])], H)

            def route_tokens(b):
                for i in range(TT * b, TT * b + TT):
                    if i % 4 == 0:
                        pe.wait_ge(x1t_read, 2 * (i // 4) + 2)
                    for c in range(KC):
                        last = mm(ps[:, 2, E * i:E * i + E], x1T[:, c, P * i:P * i + P], gwT[:, c, :], start=c == 0, stop=c == KC - 1)
                return last

            pe.wait_ge(consts, CONSTS)
            pe.wait_ge(moe_in, 16)
            for n in range(2 * NT // 4):
                i0, c = 4 * (n // KC), n % KC
                if n % (TT // 2) == 0:
                    pe.wait_ge(x1_done, n // (TT // 2) + 1)
                if n >= 2:
                    pe.wait_ge(x1t_read, n - 1)
                for s in range(4):
                    last = nc.tensor.transpose(ps[:, n % 2, P * s:P * s + P], yacc[:, i0 + s, P * c:P * c + P], ident[:, :])
                last.then_inc(x1t_done, 1)
                if n % (TT // 2) == TT // 2 - 1:
                    last = route_tokens(n // (TT // 2))
            last.then_inc(logit_done, 1)

            def shared_up(n):
                tc, (f0, fn) = n // 3, SFC[n % 3]
                if n >= 2:
                    pe.wait_ge(gu_read, n - 1)
                for u in range(2):
                    for k in range(KC):
                        last = mm(ps[0:fn, 4 + 2 * (n % 2) + u, :], wsgu[:, k, SI * u + f0:SI * u + f0 + fn],
                                  x1T[:, k, 512 * tc:512 * tc + 512], start=k == 0, stop=k == KC - 1)
                last.then_inc(gu_done, 1)

            def shared_down(i):
                if i % 4 == 0:
                    pe.wait_ge(act_done, 3 * (i // 4) + 3)
                if i == 0:
                    pe.wait_ge(gu_read, SHARED_UNITS)
                if i >= 2:
                    pe.wait_ge(sd_read, i - 1)
                for c, (f0, fn) in enumerate(SFC):
                    last = mm(ps[:, 4 + i % 2, 0:D], actS[0:fn, c, P * i:P * i + P], wsd[0:fn, c, :], start=c == 0, stop=c == 2)
                last.then_inc(sd_done, 1)

            pe.wait_ge(moe_in, 16 * 5)
            for n in range(SHARED_FIRST):
                shared_up(n)
            pe.wait_ge(sel_done, 1)
            for i in range(NT):
                last = mm(ps[:, 3, E * i:E * i + E], tri[:, :], sel[:, PAD + i, :], start=True, stop=i == 0)
                if i:
                    last = mm(ps[:, 3, E * i:E * i + E], onesb[:, :], cum[1][:, PAD + i - 1, :], start=False, stop=True)
            last.then_inc(pos_done, 1)
            for n in range(SHARED_FIRST, SHARED_SECOND):
                shared_up(n)
            pe.wait_ge(info_in, 1)
            for i in range(NT):
                pe.wait_ge(onehot_done, i + 1)
                for q in range(3):
                    last = mm(ps[0:NI, q, :], info[:, i, :], onehot[:, i, 512 * q:512 * q + 512], start=i == 0, stop=i == NT - 1)
            last.then_inc(infot_done, 1)
            shared_up(SHARED_SECOND)
            for m in range(SC):
                if m % 4 == 0:
                    pe.wait_ge(minfo_done, m // 4 + 1)
                last = mm(ps[:, 3, 3 * m:3 * m + 3], minfo[0:NI, P * m:P * m + P], slotsel[0:NI, :], start=True, stop=True)
            last.then_inc(slot_done, 1)
            for n in range(SHARED_SECOND + 1, SHARED_UNITS):
                shared_up(n)
            for i in range(4):
                shared_down(i)
            for n in range(3 * KC):
                q, c = n // KC, n % KC
                if c == 0:
                    pe.wait_ge(xg_in[q], 16 * 4)
                if n >= 2:
                    pe.wait_ge(xbt_read, n - 1)
                for s in range(4):
                    last = nc.tensor.transpose(ps[:, n % 2, P * s:P * s + P], xg[:, 4 * q + s, P * c:P * c + P], ident[:, :])
                last.then_inc(xbt_done, 1)
                for i in range(4 + 2 * n, 6 + 2 * n):
                    shared_down(i)

            def gate_up(g, k):
                pe.wait_ge(ew_in[k], g * 32 + 32)
                pe.wait_ge(eact_done, g * EB + k + 1)
                for f in range(4):
                    for c in range(KC):
                        last = mm(ps[0:FH, 4 + k % 2, C * f:C * f + C], wgu[:, k, c, FH * f:FH * f + FH],
                                  xbT[:, c, bass.ds(g * (EB * C) + k * C, C)], start=c == 0, stop=c == KC - 1)
                last.then_inc(egu_done, 1)

            def expert_down(g, k):
                pe.wait_ge(eact_done, g * EB + k + 3)
                pe.wait_ge(ey_evac, g * EB + k + 1)
                for u in range(2):
                    last = mm(ps[0:C, 6 + k % 2, 0:D], actE[0:FH, k % 2, u, :], wd[:, k, u, :], start=u == 0, stop=u == 1)
                last.then_inc(ey_done, 1)

            pe.wait_ge(xbt_read, 3 * KC)
            pe.wait_ge(sd_read, NT)
            gate_up(0, 0)
            with pe.Fori(0, TURNS - 1) as g:
                for k in range(EB):
                    gate_up(g + (k + 1) // EB, (k + 1) % EB)
                    expert_down(g, k)
            for k in range(EB):
                if k + 1 < EB:
                    gate_up(TURNS - 1, k + 1)
                expert_down(TURNS - 1, k)
            def combine(i, m0, m1):
                for m in range(m0, m1):
                    mm(ps[:, i % 4, 0:D], ohT[:, i, m, :], y_hi[:, m, :], start=m == 0, stop=False)
                    last = mm(ps[:, i % 4, 0:D], ohT[:, i, m, :], y_lo[:, m, :], start=False, stop=m == SC - 1)
                if m1 == SC:
                    last.then_inc(comb_done, 1)

            early = SC - ECH
            pe.wait_ge(ylo_done, TURNS - 1)
            for i in range(4):
                pe.wait_ge(oht_done, 2 * i + 2)
                combine(i, 0, early)
            pe.wait_ge(ylo_done, TURNS)
            for i in range(4):
                combine(i, early, SC)
            for i in range(4, NT):
                pe.wait_ge(oht_done, 2 * i + 2)
                pe.wait_ge(comb_free, i - 3)
                combine(i, 0, SC)

        @block.scalar
        def _(act):
            for first in (tanh_done, *yb_in):
                act.sem_inc(first, 1)
            act.sem_inc(ey_evac, 2)

            act.dma_start(xraw[:, 1, 0:T], xT_d[P:D, 0:T]).then_inc(xT_in[0], 16)
            for dst_, src_ in ((gtmp[:, 0, :], cos_d), (gtmp[:, 1, :], sin_d), (nrm[:, 0, :], qn), (nrm[:, 1, :], kn)):
                act.dma_start(dst_, src_).then_inc(small_in, 16)

            def copy_hi(dst, src):
                return nc.scalar.activation(dst, src, ACT.Copy)

            for b in range(B):
                act.wait_ge(xT_in[b], 16 * KC)
                copy_hi(xT[0][:, :, b * T:b * T + T], xraw[:, :, b * T:b * T + T]).then_inc(xhi_done, 1)

            def projected(what, b, count, bank_no):
                if what == "q":
                    act.wait_ge(pj_free, count)
                    nc.scalar.activation(qsq[:, :], qraw[:, :], ACT.Square).then_inc(sq_done, 1)
                    return
                act.wait_ge(pj_done, count)
                bank = ps[:, bank_no, :]
                cols = slice(512 * int(what[1]), 512 * int(what[1]) + 512)
                if what[0] == "k":
                    nc.scalar.activation(ksq[:, cols], bank, ACT.Square).then_inc(sq_done, 1)
                copy_hi((kT if what[0] == "k" else vS)[0][:, b, cols], bank).then_inc(kvhi_done, 1)

            for n, what in enumerate(PROLOGUE):
                if what == "q1":
                    projected("q", 0, n + 1, None)
                elif what[0] in "kv":
                    projected(what, 0, n + 1, PJ + n % 2)

            def tanh(s, b, j):
                t = s * TT + j
                act.wait_ge(s_ready, t + 1)
                if j == 0:
                    act.wait_ge(r_done, s + 1)
                act.wait_ge(pacc_done, t + (2 if j == RING else 1))
                act.wait_ge(plo_done, t + 1)
                buf = ps[:, 2 * (j % 2):2 * (j % 2) + 2, :].rearrange("p k n -> p (k n)")
                nc.scalar.activation(praw[:, j % RING, 0:T - P * j], buf[:, P * j:T], ACT.Tanh,
                                     scale=rstd[:, b, TT + j:TT + j + 1]).then_inc(tanh_done, 1)

            def exp(s, j):
                act.wait_ge(tanh_done, s * TT + j + 2)
                tile = praw[:, j % RING, 0:T - P * j]
                nc.scalar.activation(tile, tile, ACT.Exp, scale=CAP).then_inc(exp_done, 1)

            def hi(s, j):
                act.wait_ge(mask_done, s * TT + j + 1)
                act.wait_ge(pv_done, s * TT + j + 1)
                copy_hi(prob[0][:, j % RING, 0:T - P * j], praw[:, j % RING, 0:T - P * j]).then_inc(phi_done, 1)

            def run(hd, steps, h):
                for b, step in steps:
                    s = h * B + b
                    for k in step:
                        prev = k.endswith("'")
                        if k[0] == "t":
                            tanh(s, b, int(k[1]))
                        elif k[0] == "e":
                            exp(s - prev, int(k[1]))
                        elif k[0] == "h":
                            hi(s - prev, int(k[1]))
                        elif k == "O":
                            act.wait_ge(pv_done, s * TT + RING)
                            copy_hi(oT[0][:, :], ps[:, 4:6, :].rearrange("p k n -> p (k n)")).then_inc(ohi_done, 1)
                        elif k == "q":
                            projected(k, 1 - b, *hd.unit(b, "q1"))
                        else:
                            projected(k, 1 - b, *hd.unit(b, k))

            def head(h, kind):
                hd = Head(h, kind)
                run(hd, hd.steps(ACT_STEP), h)

            head(0, "first")
            with act.Fori(1, H - 1) as h:
                head(h, "middle")
            head(H - 1, "last")
            run(Head(H, "tail"), [(0, TAIL["act"])], H)

            act.wait_ge(pj_free, UNITS_ALL)
            for n in range(2 * NT // 4):
                act.wait_ge(x1t_done, n + 1)
                nc.scalar.activation(x1T[:, n % KC, 512 * (n // KC):512 * (n // KC) + 512], ps[:, n % 2, :], ACT.Copy).then_inc(x1t_read, 1)

            def shared_halves(n):
                fn = SFC[n % 3][1]
                act.wait_ge(gu_done, n + 1)
                if n >= SR:
                    act.wait_ge(act_done, n - SR + 1)
                nc.scalar.activation(silu_s[0:fn, n % SR, :], ps[0:fn, 4 + 2 * (n % 2), :], ACT.Silu)
                nc.scalar.activation(up_s[0:fn, n % SR, :], ps[0:fn, 5 + 2 * (n % 2), :], ACT.Copy).then_inc(gu_read, 1)

            for n in range(2):
                shared_halves(n)
            act.wait_ge(diff_done, 1)
            nc.scalar.activation(wts[:, :, :], wts[:, :, :], ACT.Exp).then_inc(e_done, 1)
            for n in range(2, SHARED_UNITS):
                shared_halves(n)
            for i in range(NT):
                act.wait_ge(sd_done, i + 1)
                if i >= 2:
                    act.wait_ge(sd_added, i - 1)
                nc.scalar.activation(sdown[:, i % 2, :], ps[:, 4 + i % 2, 0:D], ACT.Copy).then_inc(sd_read, 1)

            def expert_silu(g, k):
                act.wait_ge(egu_done, g * EB + k + 1)
                nc.scalar.activation(silE[0:FH, k % 2, :], ps[0:FH, 4 + k % 2, 0:2 * C], ACT.Silu).then_inc(esil_done, 1)

            def expert_out(g, k):
                act.wait_ge(ey_done, g * EB + k + 1)
                act.wait_ge(yb_in[k % 4], g * YB_TURN[k % 4] + YB_BEFORE[k] + 1)
                nc.scalar.activation(ye[0:C, k % 4, :], ps[0:C, 6 + k % 2, 0:D], ACT.Copy).then_inc(ey_evac, 1)
                act.wait_ge(ey_evac, g * EB + k + 3)
                for r0, p0, ch, rows in expert_pieces(k):
                    act.dma_start(ybuf[p0:p0 + rows, bass.ds(g * ECH + ch, 1), :].rearrange("p o d -> p (o d)"),
                                  ye[r0:r0 + rows, k % 4, :]).then_inc(yb_in[k % 4], 16)

            expert_silu(0, 0)
            with act.Fori(0, TURNS - 1) as g:
                for k in range(EB):
                    expert_silu(g + (k + 1) // EB, (k + 1) % EB)
                    expert_out(g, k)
            for k in range(EB):
                if k + 1 < EB:
                    expert_silu(TURNS - 1, k + 1)
                expert_out(TURNS - 1, k)
            for i in range(NT):
                act.wait_ge(norm_done, i + 1)
                act.dma_start(out_v[:, i, :], yacc[:, i, :]).then_inc(out_done, 16)

        @block.gpsimd
        def _(pool):
            nc.gpsimd.memset(ones[:, :], 1.0).then_inc(consts, 1)
            nc.gpsimd.memset(mhalf[:, :], -0.5).then_inc(consts, 1)
            nc.gpsimd.memset(causal[:, :], 1.0).then_inc(consts, 1)
            pool.wait_ge(consts, 3)
            nc.gpsimd.affine_select(out=causal[:, :], in_=causal[:, :], compare_op=ALU.is_ge, fill=0.0, base=0,
                                    pattern=[[1, P]], channel_multiplier=-1).then_inc(consts, 1)
            g_ = nc.gpsimd
            g_.memset(ident[:, :], 0.0).then_inc(consts, 1)
            g_.memset(tri[:, :], 1.0).then_inc(consts, 1)
            g_.memset(onesb[:, :], 1.0).then_inc(consts, 1)
            g_.memset(slotsel[:, :], 0.0).then_inc(consts, 1)
            g_.iota(iota48[:, :], pattern=[[1, C]], base=0, channel_multiplier=0,
                    allow_small_or_imprecise_dtypes=True).then_inc(consts, 1)
            pool.wait_ge(consts, 9)
            g_.affine_select(out=ident[:, :], in_=ident[:, :], compare_op=ALU.not_equal, fill=1.0, base=0,
                             pattern=[[1, P]], channel_multiplier=-1).then_inc(consts, 1)
            g_.affine_select(out=tri[:, :], in_=tri[:, :], compare_op=ALU.is_gt, fill=0.0, base=0,
                             pattern=[[1, P]], channel_multiplier=-1).then_inc(consts, 1)
            g_.memset(slotsel[0:3 * E, 0:1], 1.0).then_inc(consts, 1)
            rest = slotsel[3 * E:NI, :]
            for row, col, value in ((0, 1, 1.0), (1, 1, float(P)), (2, 2, 1.0)):
                pool.wait_ge(consts, 12 + row)
                g_.affine_select(out=rest[:, col:col + 1], in_=rest[:, col:col + 1], compare_op=ALU.not_equal, fill=value,
                                 base=-row, pattern=[[0, 1]], channel_multiplier=1).then_inc(consts, 1)
            pool.wait_ge(consts, CONSTS)
            pool.wait_ge(g_done, 5)
            def rms(b, count):
                pool.wait_ge(pj_free, count)
                nc.gpsimd.tensor_tensor(rstd[:, b, :], var[:, b, :], mhalf[:, :], ALU.pow).then_inc(r_done, 1)

            pool.sem_inc(pacc_done, RING)
            nc.gpsimd.tensor_copy(gcur[:, :], ghead[:, 0:1]).then_inc(gcur_done, 1)
            rms(0, PROLOGUE.index("ss") + 1)

            def tile(s, b, j):
                t = s * TT + j
                pool.wait_ge(exp_done, t + 1)
                diag = praw[:, j % RING, 0:P]
                nc.gpsimd.tensor_tensor(diag, diag, causal[:, :], ALU.mult).then_inc(mask_done, 1)
                pool.wait_ge(mask_done, t + 1)
                raw = praw[:, j % RING, 0:T - P * j]
                if j == 0:
                    pool.sem_inc(waited, 1)
                    nc.gpsimd.tensor_copy(pacc[:, b, 0:P], raw[:, 0:P]).then_inc(pacc_done, 1)
                else:
                    before = praw[:, 0, P:T] if j == 1 else pacc[:, b, P * j:T]
                    pool.wait_ge(pacc_done, t + RING)
                    nc.gpsimd.tensor_tensor(pacc[:, b, P * j:T], before, raw, ALU.add).then_inc(pacc_done, 1)

            def run(hd, steps, h):
                for b, step in steps:
                    s = h * B + b
                    for k in step:
                        if k[0] == "m":
                            prev = k.endswith("'")
                            tile(s - prev, (b + prev) % B, int(k[1]))
                        elif k == "ss":
                            rms(1 - b, hd.unit(b, k)[0])
                        elif k == "g" and b == 1:
                            pool.wait_ge(qf_done, s + 1)
                            pool.sem_inc(waited, 1)
                            nc.gpsimd.tensor_copy(gcur[:, :], ghead[:, bass.ds(h + 1, 1)]).then_inc(gcur_done, 1)

            def head(h, kind):
                hd = Head(h, kind)
                run(hd, hd.steps(POOL_STEP), h)

            head(0, "first")
            with pool.Fori(1, H - 1) as h:
                head(h, "middle")
            head(H - 1, "last")
            run(Head(H, "tail"), [(0, TAIL["pool"])], H)
            def layernorm_rstd(b):
                pool.wait_ge(var1, b + 1)
                nc.gpsimd.tensor_tensor(lnr[:, TT * b:TT * b + TT], lnv[:, TT * b:TT * b + TT], mhalf[:, 0:TT], ALU.pow).then_inc(rln1, 1)

            layernorm_rstd(0)
            pool.wait_ge(pj_free, UNITS_ALL)
            for t in (sel, *cum):
                nc.gpsimd.memset(t[:, 0:PAD, :], 0.0).then_inc(pads, 1)
            nc.gpsimd.memset(grp[:, :, G:G + 5], NEG).then_inc(pads, 1)
            nc.gpsimd.memset(mk[:, :, E:E + 2], NEG).then_inc(pads, 1)
            layernorm_rstd(1)
            nc.gpsimd.iota(iota128[:, :], pattern=[[1, P]], base=0, channel_multiplier=0,
                           allow_small_or_imprecise_dtypes=True).then_inc(pads, 1)
            nc.gpsimd.memset(emask[:, :], 1.0).then_inc(pads, 1)
            nc.gpsimd.iota(tile0[:, :, :], pattern=[[P, NT], [0, SC]], base=0, channel_multiplier=0,
                    allow_small_or_imprecise_dtypes=True).then_inc(pads, 1)
            nc.gpsimd.iota(info[:, :, 3 * E:3 * E + 1], pattern=[[0, NT], [0, 1]], base=0, channel_multiplier=1,
                    allow_small_or_imprecise_dtypes=True).then_inc(pads, 1)
            nc.gpsimd.iota(info[:, :, 3 * E + 1:3 * E + 2], pattern=[[1, NT], [0, 1]], base=0, channel_multiplier=0,
                    allow_small_or_imprecise_dtypes=True).then_inc(pads, 1)
            nc.gpsimd.memset(info[:, :, 3 * E + 2:3 * E + 4], 1.0).then_inc(pads, 1)
            pool.wait_ge(pads, 11)
            for part in range(3):
                rows = emask[E * part:E * part + E, :].rearrange("p (e c) -> p e c", c=C)
                nc.gpsimd.affine_select(out=rows, in_=rows, compare_op=ALU.is_equal, fill=0.0, base=0,
                                 pattern=[[1, E], [0, C]], channel_multiplier=-1).then_inc(pads, 1)

            pool.wait_ge(pads, 14)

            def shared_product(n):
                c, fn, tc = n % 3, SFC[n % 3][1], n // 3
                pool.wait_ge(gu_read, n + 1)
                nc.gpsimd.tensor_tensor(actS[0:fn, c, 512 * tc:512 * tc + 512], silu_s[0:fn, n % SR, :], up_s[0:fn, n % SR, :],
                                        ALU.mult).then_inc(act_done, 1)

            def apart(i):
                nc.gpsimd.tensor_tensor(onehot[:, i, :].rearrange("p (e c) -> p e c", c=C),
                                        posb[:, i, :].unsqueeze(2).to_broadcast([P, E, C]),
                                        iota48[:, :].unsqueeze(1).to_broadcast([P, E, C]), ALU.subtract).then_inc(apart_done, 1)

            for n in range(SHARED_FIRST):
                shared_product(n)
            pool.wait_ge(posb_done, 1)
            for k in range(len(HELPED)):
                apart(HELPED[k])
                if SHARED_FIRST + k <= SHARED_SECOND:
                    shared_product(SHARED_FIRST + k)
            for n in range(SHARED_FIRST + len(HELPED), SHARED_SECOND + 1):
                shared_product(n)
            pool.wait_ge(tok_done, 1)
            pool.wait_ge(x1_out, 16 * B)
            for m in range(SC):
                nc.gpsimd.indirect_dma_start(xg[:, m, :], None, x1_d, bass.IndirectOffsetOnAxis(ap=toki[:, m:m + 1], axis=0)).then_inc(xg_in[m // 4], 16)
            for n in range(SHARED_SECOND + 1, SHARED_UNITS):
                shared_product(n)
            for i in range(NT):
                pool.wait_ge(sd_read, i + 1)
                nc.gpsimd.tensor_tensor(yacc[:, i, :], yacc[:, i, :], sdown[:, i % 2, :], ALU.add).then_inc(sd_added, 1)
            for i in range(NT):
                pool.wait_ge(var2, i + 1)
                nc.gpsimd.tensor_tensor(lnr[:, i:i + 1], lnv[:, i:i + 1], mhalf[:, 0:1], ALU.pow).then_inc(rln2, 1)

        @block.vector
        def _(dve):
            v = nc.vector
            dve.sem_inc(o_evac, 1)
            dve.sem_inc(eact_done, 2)
            dve.sem_inc(plo_done, RING)

            def lo_of(dst, x_, hi, done):
                v.tensor_tensor(dst, x_, hi.bitcast(F32), ALU.subtract).then_inc(done, 1)

            ALL = slice(None)

            def split_x(b):
                cols = slice(b * T, b * T + T)
                lo_of(xT[1][:, :, cols], xraw[:, :, cols], xT[0][:, :, cols], xlo_done)

            def split(pair_, at_, src, hi_sem, n, lo_sem):
                v.tensor_copy(pair_[0][at_], src).then_inc(hi_sem, 1)
                dve.wait_ge(hi_sem, n)
                lo_of(pair_[1][at_], src, pair_[0][at_], lo_sem)

            dve.wait_ge(w_in, 16)
            split(wqk, (ALL,) * 4, wraw[:, :, :, :], whi_done, 1, wlo_done)
            dve.wait_ge(xhi_done, 1)
            split_x(0)
            dve.wait_ge(small_in, 64)
            v.tensor_tensor(gtmp[:, 2, :], gtmp[:, 0, :], gtmp[:, 0, :], ALU.mult).then_inc(g_done, 1)
            v.tensor_tensor(gtmp[:, 3, :], gtmp[:, 1, :], gtmp[:, 1, :], ALU.mult).then_inc(g_done, 1)
            v.tensor_tensor(nrm[:, 2, :], nrm[:, 0, :], nrm[:, 1, :], ALU.mult).then_inc(g_done, 1)
            dve.wait_ge(g_done, 3)
            v.tensor_tensor(gtmp[:, 2, :], gtmp[:, 2, :], gtmp[:, 3, :], ALU.add).then_inc(g_done, 1)
            dve.wait_ge(g_done, 4)
            v.tensor_scalar(ghead[:, :], gtmp[:, 2, :], nrm[:, 2, :], DH ** -0.5 / CAP, ALU.mult, ALU.mult).then_inc(g_done, 1)
            dve.wait_ge(xhi_done, 2)
            split_x(1)
            dve.wait_ge(x_in, 16)

            def projected(what, b, step, count, bank_no):
                dve.wait_ge(pj_done, count)
                bank = ps[:, bank_no, :]
                if what == "ss":
                    v.tensor_scalar(var[:, b, :], bank[:, 0:2 * TT], 1.0 / DH, RMS_EPS, ALU.mult, ALU.add).then_inc(pj_free, 1)
                    return
                cols = slice(512 * int(what[1]), 512 * int(what[1]) + 512)
                if what[0] == "q":
                    if what == "q0" and not (isinstance(step, int) and step == 0):
                        dve.wait_ge(qlo_done, step)
                    v.tensor_copy(qraw[:, cols], bank).then_inc(pj_free, 1)
                    return
                dve.wait_ge(kvhi_done, step * 4 + ["k0", "k1", "v0", "v1"].index(what) + 1)
                dst = kT if what[0] == "k" else vS
                lo_of(dst[1][:, b, cols], bank, dst[0][:, b, cols], pj_free)

            def scale_queries(step, b):
                dve.wait_ge(rqB_in, step * 16 + 16)
                v.scalar_tensor_tensor(qraw[:, :], qraw[:, :], gcur[:, :], rqB[:, :], ALU.mult, ALU.mult).then_inc(qf_done, 1)
                dve.wait_ge(qf_done, step + 1)
                split(qhat, (ALL, b, ALL), qraw[:, :], qhi_done, step + 1, qlo_done)

            for n, what in enumerate(PROLOGUE):
                projected(what, 0, 0, n + 1, PJ + n % 2)
            dve.wait_ge(gcur_done, 1)
            scale_queries(0, 0)

            def tile(s, j):
                dve.wait_ge(phi_done, s * TT + j + 1)
                n = T - P * j
                lo_of(prob[1][:, j % RING, 0:n], praw[:, j % RING, 0:n], prob[0][:, j % RING, 0:n], plo_done)

            def out_projected(b, u, sums_count, count, bank_no):
                if u == 0:
                    dve.wait_ge(pj_free, sums_count)
                dve.wait_ge(pj_done, count)
                for i in range(2):
                    y = yacc[:, b * TT + 2 * u + i, :]
                    last = v.scalar_tensor_tensor(y, ps[:, bank_no, D * i:D * i + D], rsum[:, b, 2 * u + i:2 * u + i + 1], y,
                                                  ALU.mult, ALU.add)
                last.then_inc(pj_free, 1)

            def run(hd, steps, h):
                for b, step in steps:
                    s = h * B + b
                    for k in step:
                        if k[0] == "l":
                            tile(s - k.endswith("'"), int(k[1]))
                        elif k == "O":
                            dve.wait_ge(ohi_done, s)
                            lo_of(oT[1][:, :], ps[:, 4:6, :].rearrange("p k n -> p (k n)"), oT[0][:, :], o_evac)
                        elif k == "sums":
                            count, bank_no = hd.unit(b, k)
                            dve.wait_ge(pj_done, count)
                            v.reciprocal(rsum[:, 1 - b, :], ps[:, bank_no, 0:TT]).then_inc(pj_free, 1)
                        elif k[:2] == "op":
                            out_projected(1 - b, int(k[2]), hd.unit(b, "sums")[0], *hd.unit(b, k))
                        elif k == "wo":
                            if b == 1:
                                dve.wait_ge(wo_in, h * 16 + 16)
                                if not hd.first:
                                    dve.wait_ge(pj_done, hd.unit(0, "op3")[0])
                                split(wo, (ALL, ALL), woraw[:, :], wohi_done, h + 1, wolo_done)
                        elif k == "wqk":
                            if b == 0 and not hd.last:
                                dve.wait_ge(w_in, h * 16 + 32)
                                dve.wait_ge(pj_done, hd.unit(0, "k1")[0])
                                split(wqk, (ALL,) * 4, wraw[:, :, :, :], whi_done, h + 2, wlo_done)
                        elif k == "qf":
                            if b == 1:
                                dve.wait_ge(gcur_done, h + 2)
                            scale_queries(s + 1, 1 - b)
                        else:
                            projected(k, 1 - b, s + 1, *hd.unit(b, k))
                            if k == "v1" and b == 0:
                                dve.sem_inc(wv_free, 1)

            def head(h, kind):
                hd = Head(h, kind)
                run(hd, hd.steps(DVE_STEP), h)

            head(0, "first")
            with dve.Fori(1, H - 1) as h:
                head(h, "middle")
            head(H - 1, "last")
            steps = [0]

            def step(ins):
                steps[0] += 1
                ins.then_inc(dstep, 1)

            def settle():
                dve.wait_ge(dstep, steps[0])

            def layernorm_stats(b):
                for i in range(TT * b, TT * b + TT):
                    step(v.bn_stats(stats[:, i, :], yacc[:, i, :]))
                settle()
                for i in range(TT * b, TT * b + TT):
                    step(v.bn_aggr(mv[:, i, :], stats[:, i, :]))
                settle()
                v.tensor_scalar(lnv[:, TT * b:TT * b + TT], mv[:, TT * b:TT * b + TT, 1], LN_EPS, None, ALU.add).then_inc(var1, 1)

            def normalise(i):
                return v.tensor_scalar(yacc[:, i, :], yacc[:, i, :], mv[:, i, 0:1], lnr[:, i:i + 1], ALU.subtract, ALU.mult)

            at_ = TAIL["dve"].index("sums")
            run(Head(H, "tail"), [(0, TAIL["dve"][:at_])], H)
            layernorm_stats(0)
            run(Head(H, "tail"), [(0, TAIL["dve"][at_:])], H)
            dve.wait_ge(pj_free, UNITS_ALL)
            for b in range(B):
                if b:
                    layernorm_stats(b)
                dve.wait_ge(rln1, b + 1)
                for i in range(TT * b, TT * b + TT):
                    ins = normalise(i)
                ins.then_inc(x1_done, 1)

            dve.wait_ge(consts, CONSTS)
            dve.wait_ge(pads, 5)
            dve.wait_ge(logit_done, 1)
            step(v.tensor_copy(lg[:, :, :].rearrange("p i e -> p (i e)"), ps[:, 2, :]))
            settle()
            step(v.tensor_reduce(grp[:, :, 0:G], lg[:, :, :].rearrange("p i (g e) -> p i g e", e=EG), AX, ALU.max))
            settle()
            for i in range(NT):
                step(v.max(g8[:, i, :], grp[:, i, 0:G]))
            settle()
            step(v.memset(g8[:, :, TOPG:8], NEG))
            settle()
            for i in range(NT):
                step(v.match_replace(grep[:, i, :], g8[:, i, :], grp[:, i, :], POS))
            settle()
            step(v.tensor_tensor(keep[:, :, :], grep[:, :, 0:G], grp[:, :, 0:G], ALU.not_equal))
            settle()
            step(v.tensor_tensor(lg[:, :, :].rearrange("p i (g e) -> p (i g) e", e=EG),
                                 lg[:, :, :].rearrange("p i (g e) -> p (i g) e", e=EG),
                                 keep[:, :, :].rearrange("p i g -> p (i g)").unsqueeze(2).to_broadcast([P, NT * G, EG]), ALU.mult))
            settle()
            step(v.tensor_scalar(mk[:, :, 0:E], lg[:, :, :], 0.0, None, ALU.add))
            settle()
            for i in range(NT):
                step(v.max(m8[:, i, :], mk[:, i, 0:E]))
            settle()
            v.tensor_tensor(wts[:, :, :], mk[:, :, 0:E], m8[:, :, 0:1].to_broadcast([P, NT, E]), ALU.subtract).then_inc(diff_done, 1)
            dve.wait_ge(diff_done, 1)
            step(v.memset(m8[:, :, TOPK:8], NEG))
            settle()
            for i in range(NT):
                step(v.match_replace(mrep[:, i, :], m8[:, i, :], mk[:, i, :], POS))
            settle()
            step(v.tensor_tensor(sel[:, PAD:PAD + NT, :], mrep[:, :, 0:E], mk[:, :, 0:E], ALU.not_equal))
            src = sel
            for k, span in enumerate((1, 2, 4, 8)):
                settle()
                dst = cum[k % 2]
                ins = v.tensor_tensor(dst[:, PAD:PAD + NT, :], src[:, PAD:PAD + NT, :], src[:, PAD - span:PAD + NT - span, :], ALU.add)
                src = dst
                if span < 8:
                    step(ins)
            ins.then_inc(sel_done, 1)
            step(v.tensor_scalar(posm[:, :, :], sel[:, PAD:PAD + NT, :], -4096.0, 4096.0, ALU.mult, ALU.add))
            dve.wait_ge(pos_done, 1)
            settle()
            v.tensor_tensor(posb[:, :, :].rearrange("p i e -> p (i e)"), posm[:, :, :].rearrange("p i e -> p (i e)"), ps[:, 3, :], ALU.add).then_inc(posb_done, 1)
            dve.wait_ge(pads, 14)
            dve.wait_ge(e_done, 1)
            step(v.tensor_reduce(srow[:, :], wts[:, :, :], AX, ALU.add))
            settle()
            step(v.reciprocal(rrow[:, :], srow[:, :]))
            settle()
            step(v.tensor_scalar(rrow[:, :], rrow[:, :], ROUTE_SCALE, None, ALU.mult))

            def place(i):
                if i in HELPED:
                    dve.wait_ge(apart_done, HELPED.index(i) + 1)
                    v.tensor_scalar(onehot[:, i, :], onehot[:, i, :], 0.0, None, ALU.is_equal).then_inc(onehot_done, 1)
                    return
                v.tensor_tensor(onehot[:, i, :].rearrange("p (e c) -> p e c", c=C),
                                posb[:, i, :].unsqueeze(2).to_broadcast([P, E, C]),
                                iota48[:, :].unsqueeze(1).to_broadcast([P, E, C]), ALU.is_equal).then_inc(onehot_done, 1)

            dve.wait_ge(posb_done, 1)
            place(0)
            settle()
            step(v.tensor_tensor(wts[:, :, :], wts[:, :, :], rrow[:, :].unsqueeze(2).to_broadcast([P, NT, E]), ALU.mult))
            place(1)
            settle()
            step(v.tensor_copy(info[:, :, 0:E], wts[:, :, :]))
            place(2)
            settle()
            step(v.tensor_tensor(wrest[:, :, :], wts[:, :, :], info[:, :, 0:E], ALU.subtract))
            place(3)
            settle()
            step(v.tensor_copy(info[:, :, E:2 * E], wrest[:, :, :]))
            place(4)
            settle()
            step(v.tensor_tensor(wrest[:, :, :], wrest[:, :, :], info[:, :, E:2 * E], ALU.subtract))
            place(5)
            settle()
            v.tensor_copy(info[:, :, 2 * E:3 * E], wrest[:, :, :]).then_inc(info_in, 1)
            for i in range(6, NT):
                place(i)
            dve.wait_ge(infot_done, 1)
            for q in range(3):
                v.tensor_tensor(minfo[0:NI, 512 * q:512 * q + 512], ps[0:NI, q, :], emask[0:NI, 512 * q:512 * q + 512],
                                ALU.mult).then_inc(minfo_done, 1)
            dve.wait_ge(slot_done, 1)
            slot = ps[:, 3, 0:3 * SC].rearrange("p (m n) -> p m n", n=3)
            v.tensor_copy(toki[:, :], slot[:, :, 1]).then_inc(tok_done, 1)
            step(v.tensor_scalar(tok[:, :], slot[:, :, 2], -1.0, None, ALU.add))
            step(v.tensor_copy(wslot[:, :], slot[:, :, 0]))
            settle()
            step(v.tensor_tensor(tok[:, :], tok[:, :], slot[:, :, 1], ALU.add))
            settle()
            v.tensor_tensor(tokc[:, :, :], tok[:, :].unsqueeze(1).to_broadcast([P, NT, SC]), tile0[:, :, :], ALU.subtract).then_inc(tokc_done, 1)
            for n in range(3 * KC):
                q, c = n // KC, n % KC
                dve.wait_ge(xbt_done, n + 1)
                v.tensor_copy(xbT[:, c, 512 * q:512 * q + 512], ps[:, n % 2, :]).then_inc(xbt_read, 1)

            def product(g, k):
                dve.wait_ge(esil_done, g * EB + k + 1)
                v.tensor_tensor(actE[0:FH, k % 2].rearrange("p k c -> p (k c)"), silE[0:FH, k % 2, :],
                                ps[0:FH, 4 + k % 2, 2 * C:4 * C], ALU.mult).then_inc(eact_done, 1)

            def rows(t, g, m=None):
                return t[:, bass.ds(g * ECH, ECH), :] if m is None else t[:, bass.ds(g * ECH + m, 1), :]

            def weight(g, m):
                row = rows(ybuf, g, m).rearrange("p o d -> p (o d)")
                v.tensor_scalar(row, row, wslot[:, bass.ds(g * ECH + m, 1)], None, ALU.mult).then_inc(yw_done, 1)

            def weighted_hi(g):
                dve.wait_ge(yw_done, g * ECH + ECH)
                v.tensor_copy(rows(y_hi, g), rows(ybuf, g)).then_inc(yhi_done, 1)

            def weighted_lo(g):
                dve.wait_ge(yhi_done, g + 1)
                lo_of(rows(y_lo, g), rows(ybuf, g), rows(y_hi, g), ylo_done)

            def landed(g):
                for s in range(4):
                    dve.wait_ge(yb_in[s], g * YB_TURN[s] + (YB_TURN[s] + 1))

            def tokens_of_slots(g, k):
                i, m0 = g * (EB // 2) + k // 2, SC // 2 * (k % 2)
                half = SC // 2
                v.tensor_tensor(ohT[:, bass.ds(i, 1), m0:m0 + half, :].rearrange("p o m t -> p (o m) t"),
                                tokc[:, bass.ds(i, 1), m0:m0 + half].rearrange("p o m -> p (o m)").unsqueeze(2).to_broadcast([P, half, P]),
                                iota128[:, :].unsqueeze(1).to_broadcast([P, half, P]), ALU.is_equal).then_inc(oht_done, 1)

            dve.wait_ge(sd_added, NT)
            dve.wait_ge(tokc_done, 1)
            for k in range(EB):
                product(0, k)
                tokens_of_slots(0, k)
            with dve.Fori(1, TURNS) as g:
                for k in range(EB):
                    product(g, k)
                    tokens_of_slots(g, k)
                    if k == 2:
                        landed(g - 1)
                    if 2 <= k < 2 + ECH:
                        weight(g - 1, k - 2)
                    if k == 5:
                        weighted_hi(g - 1)
                    if k == 6:
                        weighted_lo(g - 1)
            landed(TURNS - 1)
            for m in range(ECH):
                weight(TURNS - 1, m)
            weighted_hi(TURNS - 1)
            weighted_lo(TURNS - 1)

            for i in range(NT + 2):
                if i < NT:
                    dve.wait_ge(comb_done, i + 1)
                    v.tensor_tensor(yacc[:, i, :], yacc[:, i, :], ps[:, i % 4, 0:D], ALU.add).then_inc(comb_free, 1)
                if i >= 2:
                    dve.wait_ge(rln2, i - 1)
                    normalise(i - 2).then_inc(norm_done, 1)
                if i < NT:
                    dve.wait_ge(comb_free, i + 1)
                    step(v.bn_stats(stats[:, i, :], yacc[:, i, :]))
                    settle()
                    step(v.bn_aggr(mv[:, i, :], stats[:, i, :]))
                    settle()
                    v.tensor_scalar(lnv[:, i:i + 1], mv[:, i, 1:2], LN_EPS, None, ALU.add).then_inc(var2, 1)


def _yb_counts():
    turn, at_ = [0] * 4, []
    for k in range(EB):
        pieces = 1 + ((k * C) // P != ((k + 1) * C - 1) // P)
        at_.append(turn[k % 4])
        turn[k % 4] += 16 * pieces
    return turn, at_


YB_TURN, YB_BEFORE = _yb_counts()


def kernel(**inputs):
    import concourse.bacc as bacc
    from concourse.bass_utils import run_bass_kernel_spmd as run

    a = {n: np.asarray(v) for n, v in inputs.items()}
    x = a["L0_attn_x"].reshape(N, D)

    def heads(w):
        return w.reshape(H, DH, KC, P).transpose(0, 3, 2, 1)

    wqkv = np.stack([heads(a["L0_attn_wq"]), heads(a["L0_attn_wk"]), heads(a["L0_attn_wv"])], axis=2)
    wo = a["L0_attn_wo"].reshape(D, H, DH).transpose(1, 2, 0)

    def rope(t):
        return np.repeat(t[:H], 2, axis=1).T

    arrays = {
        "x": x, "xT": x.T, "wqkv": wqkv, "wo": wo,
        "qn": a["L0_attn_q_norm_w"].reshape(DH, 1), "kn": a["L0_attn_k_norm_w"].reshape(DH, 1),
        "cos": rope(a["L0_attn_rope_cos"]), "sin": rope(a["L0_attn_rope_sin"]),
        "gw": a["L0_ffn_gate_w"].T, "wgu": a["L0_ffn_w_gate_up"], "wd": a["L0_ffn_w_down"],
        "wsgu": a["L0_ffn_ws_gate_up"], "wsd": a["L0_ffn_ws_down"],
    }
    nc = bacc.Bacc("TRN2", target_bir_lowering=False, num_devices=1)
    feed, args = {}, []
    for name, arr in arrays.items():
        arr = np.ascontiguousarray(arr)
        feed[f"in_{name}"] = arr
        args.append(nc.dram_tensor(f"in_{name}", arr.shape, mybir.dt.from_np(arr.dtype), kind="ExternalInput").ap())
    args.append(nc.dram_tensor("out_0", (N, D), F32, kind="ExternalOutput").ap())
    block_kernel(nc, *args)
    r = run(nc, [feed], core_ids=[0])
    return r.results[0]["out_0"].reshape(B, T, D)
```

```python
import numpy as np
import concourse.bass as bass
from concourse import mybir
from concourse.alu_op_type import AluOpType as ALU
from contextlib import ExitStack

F32 = mybir.dt.float32
F32R = mybir.dt.float32r
BF16 = mybir.dt.bfloat16
I32 = mybir.dt.int32
ACT = mybir.ActivationFunctionType
AX = mybir.AxisListType.X

P = 128
BLK = P // 32
B, T, D = 2, 1024, 256
H, DH = 16, 128
N = B * T
NT = N // P
TT = T // P
KC = D // P
CAP = 50.0
RMS_EPS, LN_EPS = 1e-6, 1e-5
E, G, TOPG, TOPK, C = 32, 8, 3, 6, 48
EG = E // G
FI = 176
FH = FI // 2
SI = 2 * FI
SFC = [(0, 128), (128, 128), (256, 96)]
ROUTE_SCALE = 16.0
SLOTS = E * C
SC = SLOTS // P
EB = 8
ECH = EB * C // P
TURNS = E // EB
NEG = -3.0e38
POS = 3.0e38
NI = 3 * E + 4
PAD = NT // 2
HELPED = (6, 8, 10, 12, 14, 15)
SR = 2

RING = 4
PJ = 6

UNIT_ORDER = "q0 q1 k0 k1 sums op0 ss op1 v0 op2 op3 v1".split()
BEHIND = {"sums", "op0", "op1", "op2", "op3"}
PROLOGUE = "q0 q1 k0 k1 v0 v1 ss".split()


def units(b, old=True, new=True):
    return [(b, k) for k in UNIT_ORDER if (old if k in BEHIND else new)]


UNITS_FIRST = units(0, old=False) + units(1)
UNITS_HEAD = units(0) + units(1)
UNITS_LAST = units(0) + units(1, new=False)
UNITS_TAIL = units(0, new=False)
BASE1 = len(PROLOGUE) + len(UNITS_FIRST)
BASE_TAIL = BASE1 + (H - 2) * len(UNITS_HEAD) + len(UNITS_LAST)
UNITS_ALL = BASE_TAIL + len(UNITS_TAIL)


class Head:

    def __init__(self, h, kind):
        self.h = h
        self.first, self.last = kind == "first", kind == "last"
        self.units = {"first": UNITS_FIRST, "middle": UNITS_HEAD, "last": UNITS_LAST, "tail": UNITS_TAIL}[kind]
        self.base = {"first": len(PROLOGUE), "tail": BASE_TAIL}.get(kind, (h - 1) * len(UNITS_HEAD) + BASE1)
        self.parity = {"first": len(PROLOGUE), "tail": BASE_TAIL}.get(kind, BASE1) % 2

    def unit(self, b, k):
        n = self.units.index((b, k))
        return self.base + n + 1, PJ + (self.parity + n) % 2


CONSTS = 23

SHARED_UNITS = N // 512 * len(SFC)
SHARED_FIRST = 5
SHARED_SECOND = 10


def block_kernel(nc, x, xT_d, wqkv_d, wo_d, qn, kn, cos_d, sin_d, gw_d, wgu_d, wd_d, wsgu_d, wsd_d, out):
    rq_d = nc.dram_tensor("rq_rows", (B, T), F32, kind="Internal").ap()
    x1_d = nc.dram_tensor("x1_rows", (N, D), F32, kind="Internal").ap()

    ctx = ExitStack()
    with ctx:
        def sb(name, shape, dt=F32):
            return ctx.enter_context(nc.sbuf_tensor(name, shape, dt))

        def sem(name):
            return ctx.enter_context(nc.semaphore(name))

        yacc = sb("yacc", [P, NT, D])
        ones = sb("ones", [P, 2])
        causal = sb("causal", [P, P])
        mhalf = sb("mhalf", [P, 2 * TT])

        ident = sb("ident", [P, P])
        tri = sb("tri", [P, P], BF16)
        onesb = sb("onesb", [P, P], BF16)
        iota48 = sb("iota48", [P, C], BF16)
        slotsel = sb("slotsel", [P, 3])
        stats = sb("stats", [P, NT, 6])
        mv = sb("mv", [P, NT, 2])
        lnv = sb("lnv", [P, NT])
        lnr = sb("lnr", [P, NT])

        att = ExitStack()

        def asb(name, shape, dt=F32):
            return att.enter_context(nc.sbuf_tensor(name, shape, dt))

        def pair(name, shape):
            return asb(name + "_hi", shape, F32R), asb(name + "_lo", shape, F32R)

        xT = pair("xT", [P, KC, N])
        xraw = asb("xraw", [P, KC, N])
        wraw = asb("wraw", [P, 2, KC, DH])
        wqk = pair("wqk", [P, 2, KC, DH])
        wv = asb("wv", [P, KC, DH])
        woraw = asb("woraw", [P, D])
        wo = pair("wo", [P, D])
        praw = asb("praw", [P, RING, T])
        prob = pair("prob", [P, RING, T])
        pacc = asb("pacc", [P, B, T])
        qraw = asb("qraw", [P, T])
        qhat = pair("qhat", [P, B, T])
        kT = pair("kT", [P, B, T])
        vS = pair("vS", [P, B, T])
        rqB = asb("rqB", [P, T])
        oT = pair("oT", [P, T])
        qsq = asb("qsq", [P, T])
        ksq = asb("ksq", [P, T])
        fold = asb("fold", [P, P])
        sqT = asb("sqT", [P, T // 2])
        sqp = asb("sqp", [P, 2, BLK, TT])
        var = asb("var", [P, B, 2 * TT])
        rstd = asb("rstd", [P, B, 2 * TT])
        rsum = asb("rsum", [P, B, TT])
        ghead = asb("ghead", [P, H])
        gcur = asb("gcur", [P, 1])
        gtmp = asb("gtmp", [P, 4, H])
        nrm = asb("nrm", [P, 3, 1])
        att.close()

        wgu = sb("wgu", [P, EB, KC, 2 * FI])
        wd = sb("wd", [FH, EB, 2, D])
        iota128 = sb("iota128", [P, P])
        tokc = sb("tokc", [P, NT, SC])
        wslot = sb("wslot", [P, SC])
        xbT = sb("xbT", [P, KC, SLOTS])

        route = ExitStack()

        def rsb(name, shape, dt=F32):
            return route.enter_context(nc.sbuf_tensor(name, shape, dt))

        sdown = rsb("sdown", [P, 4, D])
        tile0 = rsb("tile0", [P, NT, SC])
        info = rsb("info", [P, NT, NI], BF16)
        emask = rsb("emask", [P, SLOTS])
        gwT = rsb("gwT", [P, KC, E])
        wsgu = rsb("wsgu", [P, KC, 2 * SI])
        wsd = rsb("wsd", [P, 3, D])
        x1T = rsb("x1T", [P, KC, N])
        actS = rsb("actS", [P, 3, N])
        silu_s = rsb("silu_s", [P, SR, 512])
        up_s = rsb("up_s", [P, SR, 512])
        lg = rsb("lg", [P, NT, E])
        mk = rsb("mk", [P, NT, E + 2])
        mrep = rsb("mrep", [P, NT, E + 2])
        wts = rsb("wts", [P, NT, E])
        grp = rsb("grp", [P, NT, G + 5])
        grep = rsb("grep", [P, NT, G + 5])
        keep = rsb("keep", [P, NT, G])
        m8 = rsb("m8", [P, NT, 8])
        g8 = rsb("g8", [P, NT, 8])
        srow = rsb("srow", [P, NT])
        rrow = rsb("rrow", [P, NT])
        sel = rsb("sel", [P, PAD + NT, E], BF16)
        cum = [rsb(f"cum{k}", [P, PAD + NT, E], BF16) for k in range(2)]
        posm = rsb("posm", [P, NT, E])
        posb = rsb("posb", [P, NT, E], BF16)
        wrest = posm
        tok = rsb("tok", [P, SC])
        toki = rsb("toki", [P, SC], I32)
        places = ExitStack()
        onehot = places.enter_context(nc.sbuf_tensor("onehot", [P, NT, SLOTS], BF16))
        places.close()
        minfo = rsb("minfo", [P, SLOTS])
        xg = rsb("xg", [P, SC, D])
        route.close()

        ohT = sb("ohT", [P, NT, SC, P], F32R)
        ybuf = sb("ybuf", [P, SC, D])
        y_hi = sb("y_hi", [P, SC, D], F32R)
        y_lo = sb("y_lo", [P, SC, D], F32R)
        ye = sb("ye", [P, 4, D])
        silE = sb("silE", [P, 2, 2 * C])
        actE = sb("actE", [P, 2, 2, C])

        ps = ctx.enter_context(nc.psum_tensor("ps", [P, 8, 512], F32))

        x_in = sem("x_in")
        xT_in = [sem(f"xT_in{b}") for b in range(B)]
        small_in, w_in, wv_in, wo_in = sem("small_in"), sem("w_in"), sem("wv_in"), sem("wo_in")
        consts, g_done, gcur_done = sem("consts"), sem("g_done"), sem("gcur_done")
        xhi_done, xlo_done = sem("xhi_done"), sem("xlo_done")
        whi_done, wlo_done = sem("whi_done"), sem("wlo_done")
        wohi_done, wolo_done = sem("wohi_done"), sem("wolo_done")
        pj_done, pj_free = sem("pj_done"), sem("pj_free")
        kvhi_done, qsq_done, ksq_done = sem("kvhi_done"), sem("qsq_done"), sem("ksq_done")
        folded = sem("folded")
        r_done, rq_out, rqB_in = sem("r_done"), sem("rq_out"), sem("rqB_in")
        qf_done, qhi_done, qlo_done = sem("qf_done"), sem("qhi_done"), sem("qlo_done")
        s_ready, tanh_done, exp_done = sem("s_ready"), sem("tanh_done"), sem("exp_done")
        mask_done, phi_done, plo_done = sem("mask_done"), sem("phi_done"), sem("plo_done")
        pacc_done, pv_done = sem("pacc_done"), sem("pv_done")
        ohi_done, o_evac = sem("ohi_done"), sem("o_evac")
        wv_free = sem("wv_free")
        waited = sem("waited")
        dstep = sem("dstep")
        var1, rln1, x1_done = sem("var1"), sem("rln1"), sem("x1_done")
        moe_in, x1_out = sem("moe_in"), sem("x1_out")
        x1t_done, x1t_read, pads = sem("x1t_done"), sem("x1t_read"), sem("pads")
        logit_done = sem("logit_done")
        diff_done, e_done, sel_done = sem("diff_done"), sem("e_done"), sem("sel_done")
        pos_done, info_in, onehot_done = sem("pos_done"), sem("info_in"), sem("onehot_done")
        infot_done, minfo_done, slot_done = sem("infot_done"), sem("minfo_done"), sem("slot_done")
        gu_done, gu_read, act_done = sem("gu_done"), sem("gu_read"), sem("act_done")
        sd_done, sd_read, sd_added = sem("sd_done"), sem("sd_read"), sem("sd_added")
        apart_done, posb_done = sem("apart_done"), sem("posb_done")
        tok_done, tokc_done = sem("tok_done"), sem("tokc_done")
        xg_in = [sem(f"xg_in{q}") for q in range(3)]
        xbt_done, xbt_read = sem("xbt_done"), sem("xbt_read")
        ew_in = [sem(f"ew_in{k}") for k in range(EB)]
        egu_done, esil_done, eact_done = sem("egu_done"), sem("esil_done"), sem("eact_done")
        ey_done, ey_evac = sem("ey_done"), sem("ey_evac")
        yb_in = [sem(f"yb_in{k}") for k in range(4)]
        yw_done, yhi_done, ylo_done = sem("yw_done"), sem("yhi_done"), sem("ylo_done")
        oht_done, comb_done, comb_free = sem("oht_done"), sem("comb_done"), sem("comb_free")
        var2, rln2, norm_done, out_done = sem("var2"), sem("rln2"), sem("norm_done"), sem("out_done")

        block = ctx.enter_context(nc.Block())
        x_v = x.rearrange("(i p) d -> p i d", p=P)
        x1_v = x1_d.rearrange("(i p) d -> p i d", p=P)
        out_v = out.rearrange("(i p) d -> p i d", p=P)
        wgu_v = wgu_d.rearrange("e (c p) f -> e p c f", p=P)
        wd_v = wd_d.rearrange("e (c p) n -> e p c n", p=FH)

        def expert_pieces(k):
            lo, hi = k * C, (k + 1) * C
            out_, r = [], lo
            while r < hi:
                n = min(hi, (r // P + 1) * P) - r
                out_.append((r - lo, r % P, r // P, n))
                r += n
            return out_

        @block.sync
        def _(sp):
            sp.dma_start(wraw[:, :, :, :], wqkv_d[0, :, 0:2]).then_inc(w_in, 16)
            sp.dma_start(xraw[:, 0, 0:T], xT_d[0:P, 0:T]).then_inc(xT_in[0], 16)
            sp.dma_start(wv[:, :, :], wqkv_d[0, :, 2]).then_inc(wv_in, 16)
            for c in range(KC):
                sp.dma_start(xraw[:, c, T:N], xT_d[P * c:P * c + P, T:N]).then_inc(xT_in[1], 16)
            sp.dma_start(woraw[:, :], wo_d[0]).then_inc(wo_in, 16)
            sp.dma_start(yacc[:, :, :], x_v).then_inc(x_in, 16)

            def rq_broadcast(step, b):
                sp.wait_ge(r_done, step + 1)
                sp.dma_start(rq_d[b].rearrange("(p j) -> p j", p=P), rstd[:, b, 0:TT]).then_inc(rq_out, 16)
                sp.wait_ge(rq_out, step * 16 + 16)
                sp.dma_start(rqB[:, :], rq_d[b:b + 1, :].to_broadcast([P, T])).then_inc(rqB_in, 16)

            rq_broadcast(0, 0)
            with sp.Fori(0, H - 1) as h:
                sp.wait_ge(wlo_done, h + 1)
                sp.dma_start(wraw[:, :, :, :], wqkv_d[bass.ds(h + 1, 1), :, 0:2].rearrange("o p m c d -> p (o m) c d")).then_inc(w_in, 16)
                rq_broadcast(h * B + 1, 1)
                sp.wait_ge(wv_free, h + 1)
                sp.dma_start(wv[:, :, :], wqkv_d[bass.ds(h + 1, 1), :, 2].rearrange("o p c d -> p (o c) d")).then_inc(wv_in, 16)
                sp.wait_ge(wolo_done, h + 1)
                sp.dma_start(woraw[:, :], wo_d[bass.ds(h + 1, 1)].rearrange("o p n -> p (o n)")).then_inc(wo_in, 16)
                rq_broadcast(h * B + 2, 0)
            rq_broadcast(H * B - 1, 1)

            sp.wait_ge(pj_free, UNITS_ALL)
            sp.dma_start(gwT[:, :, :], gw_d.rearrange("(c p) e -> p c e", p=P)).then_inc(moe_in, 16)
            sp.dma_start(wsgu[:, :, :], wsgu_d.rearrange("(c p) f -> p c f", p=P)).then_inc(moe_in, 16)
            for c, (f0, fn) in enumerate(SFC):
                sp.dma_start(wsd[0:fn, c, :], wsd_d[f0:f0 + fn, :]).then_inc(moe_in, 16)
            for k in range(EB):
                if k % 4 == 2:
                    sp.wait_ge(x1_done, k // 4 + 1)
                    sp.dma_start(x1_v[:, TT * (k // 4):TT * (k // 4) + TT], yacc[:, TT * (k // 4):TT * (k // 4) + TT, :]).then_inc(x1_out, 16)
                sp.dma_start(wgu[:, k], wgu_v[k]).then_inc(ew_in[k], 16)
                sp.dma_start(wd[:, k], wd_v[k]).then_inc(ew_in[k], 16)
            with sp.Fori(0, TURNS - 1) as g:
                for k in range(EB):
                    sp.wait_ge(ey_done, g * EB + k + 1)
                    sp.dma_start(wgu[:, k], wgu_v[bass.ds(g * EB + (EB + k), 1)].rearrange("o p c f -> p (o c) f")).then_inc(ew_in[k], 16)
                    sp.dma_start(wd[:, k], wd_v[bass.ds(g * EB + (EB + k), 1)].rearrange("o p c n -> p (o c) n")).then_inc(ew_in[k], 16)
            sp.wait_ge(out_done, 16 * NT)

        @block.tensor
        def _(pe):
            mm = nc.tensor.matmul
            pe.sem_inc(pv_done, RING)

            def mm3(out_, left, right, start, stop):
                mm(out_, left[0], right[0], start=start, stop=False)
                mm(out_, left[0], right[1], start=False, stop=False)
                return mm(out_, left[1], right[0], start=False, stop=stop)

            def of(pair_, *at_):
                return tuple(t[at_] for t in pair_)

            ALL = slice(None)

            def open_unit(count):
                if not isinstance(count, int) or count > 2:
                    pe.wait_ge(pj_free, count - 2)

            def project(what, b, count, bank_no):
                open_unit(count)
                bank = ps[:, bank_no, :]
                half = int(what[1])
                if what[0] in "qk":
                    m, t0 = "qk".index(what[0]), b * T + 512 * half
                    for c in range(KC):
                        last = mm3(bank, of(wqk, ALL, m, c, ALL), of(xT, ALL, c, slice(t0, t0 + 512)), c == 0, c == KC - 1)
                else:
                    for j in range(4):
                        t0 = b * T + 512 * half + P * j
                        for c in range(KC):
                            last = mm(bank[:, P * j:P * j + P], xraw[:, c, t0:t0 + P], wv[:, c, :], start=c == 0, stop=c == KC - 1)
                last.then_inc(pj_done, 1)

            def sums_of_squares(step, count, bank_no):
                open_unit(count)
                pe.wait_ge(folded, step * 8 + 8)
                mm(ps[:, bank_no, 0:2 * BLK * TT], fold[:, :], sqp[:, :, :, :].rearrange("p m g j -> p (m g j)"),
                   start=True, stop=True).then_inc(pj_done, 1)

            def scores(s, b, j):
                pe.wait_ge(tanh_done, s * TT + (1 if j == 0 else j))
                buf = ps[:, 2 * (j % 2):2 * (j % 2) + 2, :].rearrange("p k n -> p (k n)")
                for t0, t1 in ([(P * j, 512), (512, T)] if j < 4 else [(P * j, T)]):
                    last = mm3(buf[:, t0:t1], of(kT, ALL, b, slice(P * j, P * j + P)), of(qhat, ALL, b, slice(t0, t1)), True, True)
                last.then_inc(s_ready, 1)

            def values(s, b, j):
                if j == 0:
                    pe.wait_ge(o_evac, s + 1)
                pe.wait_ge(plo_done, s * TT + j + 1 + RING)
                o = ps[:, 4:6, :].rearrange("p k n -> p (k n)")
                for t0, t1 in ([(P * j, 512), (512, T)] if j < 4 else [(P * j, T)]):
                    last = mm3(o[:, t0:t1], of(vS, ALL, b, slice(P * j, P * j + P)), of(prob, ALL, j % RING, slice(t0 - P * j, t1 - P * j)),
                               j == 0, (j == 3 and t1 == 512) or j == TT - 1)
                last.then_inc(pv_done, 1)

            def sums(s, b, half, count, bank_no):
                if half == 0:
                    open_unit(count)
                    pe.wait_ge(pacc_done, (s + 1) * TT + RING)
                for j in range(TT // 2 * half, TT // 2 * half + TT // 2):
                    last = mm(ps[:, bank_no, j:j + 1], pacc[:, b, P * j:P * j + P], ones[:, 0:1], start=True, stop=True)
                if half == 1:
                    last.then_inc(pj_done, 1)

            def out_proj(s, b, u, count, bank_no):
                open_unit(count)
                if u == 0:
                    pe.wait_ge(o_evac, s + 2)
                for i in range(2):
                    t0 = P * (2 * u + i)
                    last = mm3(ps[:, bank_no, D * i:D * i + D], of(oT, ALL, slice(t0, t0 + P)), of(wo, ALL, ALL), True, True)
                last.then_inc(pj_done, 1)

            pe.wait_ge(consts, CONSTS)
            pe.wait_ge(xlo_done, 1)
            pe.wait_ge(wlo_done, 1)
            for n, what in enumerate(PROLOGUE):
                if what == "ss":
                    sums_of_squares(0, n + 1, PJ + n % 2)
                else:
                    if what == "v0":
                        pe.wait_ge(wv_in, 16)
                    project(what, 0, n + 1, PJ + n % 2)
            pe.wait_ge(xlo_done, 2)

            def step(hd, b, old=True, new=True):
                h, s = hd.h, hd.h * B + b
                if new:
                    if b == 1:
                        pe.wait_ge(wlo_done, h + 2)
                    project("q0", 1 - b, *hd.unit(b, "q0"))
                    project("q1", 1 - b, *hd.unit(b, "q1"))
                if old:
                    values(s - 1, 1 - b, 3)
                pe.wait_ge(qlo_done, s + 1)
                scores(s, b, 0)
                if new:
                    project("k0", 1 - b, *hd.unit(b, "k0"))
                if old:
                    values(s - 1, 1 - b, 4)
                if new:
                    project("k1", 1 - b, *hd.unit(b, "k1"))
                scores(s, b, 1)
                if old:
                    values(s - 1, 1 - b, 5)
                    values(s - 1, 1 - b, 6)
                    values(s - 1, 1 - b, 7)
                    sums(s - 1, 1 - b, 0, *hd.unit(b, "sums"))
                scores(s, b, 2)
                scores(s, b, 3)
                if old:
                    sums(s - 1, 1 - b, 1, *hd.unit(b, "sums"))
                    if b == 1:
                        pe.wait_ge(wolo_done, h + 1)
                    out_proj(s - 1, 1 - b, 0, *hd.unit(b, "op0"))
                scores(s, b, 4)
                if new:
                    sums_of_squares(s + 1, *hd.unit(b, "ss"))
                scores(s, b, 5)
                if old:
                    out_proj(s - 1, 1 - b, 1, *hd.unit(b, "op1"))
                if new:
                    if b == 1:
                        pe.wait_ge(wv_in, (h + 2) * 16)
                    project("v0", 1 - b, *hd.unit(b, "v0"))
                if old:
                    out_proj(s - 1, 1 - b, 2, *hd.unit(b, "op2"))
                values(s, b, 0)
                if old:
                    out_proj(s - 1, 1 - b, 3, *hd.unit(b, "op3"))
                if new:
                    project("v1", 1 - b, *hd.unit(b, "v1"))
                values(s, b, 1)
                scores(s, b, 6)
                scores(s, b, 7)
                values(s, b, 2)

            first, last = Head(0, "first"), Head(H - 1, "last")
            step(first, 0, old=False)
            step(first, 1)
            with pe.Fori(1, H - 1) as h:
                for b in range(B):
                    step(Head(h, "middle"), b)
            step(last, 0)
            step(last, 1, new=False)
            end, s = Head(H, "tail"), B * H
            for j in range(3, TT):
                values(s - 1, 1, j)
            for half in range(2):
                sums(s - 1, 1, half, *end.unit(0, "sums"))
            for u in range(4):
                out_proj(s - 1, 1, u, *end.unit(0, f"op{u}"))

            def shared_up(n):
                tc, (f0, fn) = n // 3, SFC[n % 3]
                if n >= 2:
                    pe.wait_ge(gu_read, n - 1)
                for u in range(2):
                    for k in range(KC):
                        last = mm(ps[0:fn, 4 + 2 * (n % 2) + u, :], wsgu[:, k, SI * u + f0:SI * u + f0 + fn],
                                  x1T[:, k, 512 * tc:512 * tc + 512], start=k == 0, stop=k == KC - 1)
                last.then_inc(gu_done, 1)

            def route_tokens(b):
                for i in range(TT * b, TT * b + TT):
                    if i % 4 == 0:
                        pe.wait_ge(x1t_read, 2 * (i // 4) + 2)
                    for c in range(KC):
                        last = mm(ps[:, 2, E * i:E * i + E], x1T[:, c, P * i:P * i + P], gwT[:, c, :], start=c == 0, stop=c == KC - 1)
                return last

            for n in range(2 * NT // 4):
                i0, c = 4 * (n // KC), n % KC
                if n % (TT // 2) == 0:
                    pe.wait_ge(x1_done, n // (TT // 2) + 1)
                if n >= 2:
                    pe.wait_ge(x1t_read, n - 1)
                for s in range(4):
                    last = nc.tensor.transpose(ps[:, n % 2, P * s:P * s + P], yacc[:, i0 + s, P * c:P * c + P], ident[:, :])
                last.then_inc(x1t_done, 1)
                if n == TT // 2 - 1:
                    pe.wait_ge(moe_in, 16 * 5)
                    pe.wait_ge(x1t_read, KC)
                    shared_up(0)
                if n % (TT // 2) == TT // 2 - 1:
                    last = route_tokens(n // (TT // 2))
            last.then_inc(logit_done, 1)

            def shared_down(i):
                if i % 4 == 0:
                    pe.wait_ge(act_done, 3 * (i // 4) + 3)
                if i == 0:
                    pe.wait_ge(gu_read, SHARED_UNITS)
                if i >= 2:
                    pe.wait_ge(sd_read, i - 1)
                for c, (f0, fn) in enumerate(SFC):
                    last = mm(ps[:, 4 + i % 2, 0:D], actS[0:fn, c, P * i:P * i + P], wsd[0:fn, c, :], start=c == 0, stop=c == 2)
                last.then_inc(sd_done, 1)

            for n in range(1, SHARED_FIRST):
                shared_up(n)
            pe.wait_ge(sel_done, 1)
            for i in range(NT):
                last = mm(ps[:, 3, E * i:E * i + E], tri[:, :], sel[:, PAD + i, :], start=True, stop=i == 0)
                if i:
                    last = mm(ps[:, 3, E * i:E * i + E], onesb[:, :], cum[1][:, PAD + i - 1, :], start=False, stop=True)
            last.then_inc(pos_done, 1)
            for n in range(SHARED_FIRST, SHARED_SECOND):
                shared_up(n)
            pe.wait_ge(info_in, 1)
            for i in range(NT):
                pe.wait_ge(onehot_done, i + 1)
                for q in range(3):
                    last = mm(ps[0:NI, q, :], info[:, i, :], onehot[:, i, 512 * q:512 * q + 512], start=i == 0, stop=i == NT - 1)
            last.then_inc(infot_done, 1)
            shared_up(SHARED_SECOND)
            for m in range(SC):
                if m % 4 == 0:
                    pe.wait_ge(minfo_done, m // 4 + 1)
                last = mm(ps[:, 3, 3 * m:3 * m + 3], minfo[0:NI, P * m:P * m + P], slotsel[0:NI, :], start=True, stop=True)
            last.then_inc(slot_done, 1)
            for n in range(SHARED_SECOND + 1, SHARED_UNITS):
                shared_up(n)
            for i in range(4):
                shared_down(i)
            for n in range(3 * KC):
                q, c = n // KC, n % KC
                if c == 0:
                    pe.wait_ge(xg_in[q], 16 * 4)
                if n >= 2:
                    pe.wait_ge(xbt_read, n - 1)
                for s in range(4):
                    last = nc.tensor.transpose(ps[:, n % 2, P * s:P * s + P], xg[:, 4 * q + s, P * c:P * c + P], ident[:, :])
                last.then_inc(xbt_done, 1)
                for i in range(4 + 2 * n, 6 + 2 * n):
                    shared_down(i)

            def gate_up(g, k):
                pe.wait_ge(ew_in[k], g * 32 + 32)
                pe.wait_ge(eact_done, g * EB + k + 1)
                for f in range(4):
                    for c in range(KC):
                        last = mm(ps[0:FH, 4 + k % 2, C * f:C * f + C], wgu[:, k, c, FH * f:FH * f + FH],
                                  xbT[:, c, bass.ds(g * (EB * C) + k * C, C)], start=c == 0, stop=c == KC - 1)
                last.then_inc(egu_done, 1)

            def expert_down(g, k):
                pe.wait_ge(eact_done, g * EB + k + 3)
                pe.wait_ge(ey_evac, g * EB + k + 1)
                for u in range(2):
                    last = mm(ps[0:C, 6 + k % 2, 0:D], actE[0:FH, k % 2, u, :], wd[:, k, u, :], start=u == 0, stop=u == 1)
                last.then_inc(ey_done, 1)

            pe.wait_ge(xbt_read, 3 * KC)
            pe.wait_ge(sd_read, NT)
            gate_up(0, 0)
            with pe.Fori(0, TURNS - 1) as g:
                for k in range(EB):
                    gate_up(g + (k + 1) // EB, (k + 1) % EB)
                    expert_down(g, k)
            for k in range(EB):
                if k + 1 < EB:
                    gate_up(TURNS - 1, k + 1)
                expert_down(TURNS - 1, k)
            def combine(i, m0, m1):
                for m in range(m0, m1):
                    mm(ps[:, i % 4, 0:D], ohT[:, i, m, :], y_hi[:, m, :], start=m == 0, stop=False)
                    last = mm(ps[:, i % 4, 0:D], ohT[:, i, m, :], y_lo[:, m, :], start=False, stop=m == SC - 1)
                if m1 == SC:
                    last.then_inc(comb_done, 1)

            early = SC - ECH
            pe.wait_ge(ylo_done, TURNS - 1)
            for i in range(4):
                pe.wait_ge(oht_done, 2 * i + 2)
                combine(i, 0, early)
            pe.wait_ge(ylo_done, TURNS)
            for i in range(4):
                combine(i, early, SC)
            for i in range(4, NT):
                pe.wait_ge(oht_done, 2 * i + 2)
                pe.wait_ge(comb_free, i - 3)
                combine(i, 0, SC)

        @block.scalar
        def _(act):
            for first in (tanh_done, *yb_in):
                act.sem_inc(first, 1)
            act.sem_inc(ey_evac, 2)

            act.dma_start(xraw[:, 1, 0:T], xT_d[P:D, 0:T]).then_inc(xT_in[0], 16)
            for dst_, src_ in ((gtmp[:, 0, :], cos_d), (gtmp[:, 1, :], sin_d), (nrm[:, 0, :], qn), (nrm[:, 1, :], kn)):
                act.dma_start(dst_, src_).then_inc(small_in, 16)

            def copy_hi(dst, src):
                return nc.scalar.activation(dst, src, ACT.Copy)

            for b in range(B):
                act.wait_ge(xT_in[b], 16 * KC)
                copy_hi(xT[0][:, :, b * T:b * T + T], xraw[:, :, b * T:b * T + T]).then_inc(xhi_done, 1)

            def projected(what, b, count, bank_no):
                if what == "q":
                    act.wait_ge(pj_free, count)
                    nc.scalar.activation(qsq[:, :], qraw[:, :], ACT.Square).then_inc(qsq_done, 1)
                    return
                act.wait_ge(pj_done, count)
                bank = ps[:, bank_no, :]
                cols = slice(512 * int(what[1]), 512 * int(what[1]) + 512)
                if what[0] == "k":
                    nc.scalar.activation(ksq[:, cols], bank, ACT.Square).then_inc(ksq_done, 1)
                copy_hi((kT if what[0] == "k" else vS)[0][:, b, cols], bank).then_inc(kvhi_done, 1)

            for n, what in enumerate(PROLOGUE):
                if what == "q1":
                    projected("q", 0, n + 1, None)
                elif what[0] in "kv":
                    projected(what, 0, n + 1, PJ + n % 2)

            def tanh(s, b, j):
                t = s * TT + j
                act.wait_ge(s_ready, t + 1)
                if j == 0:
                    act.wait_ge(r_done, s + 1)
                act.wait_ge(pacc_done, t + (2 if j == RING else 1))
                act.wait_ge(plo_done, t + 1)
                buf = ps[:, 2 * (j % 2):2 * (j % 2) + 2, :].rearrange("p k n -> p (k n)")
                nc.scalar.activation(praw[:, j % RING, 0:T - P * j], buf[:, P * j:T], ACT.Tanh,
                                     scale=rstd[:, b, TT + j:TT + j + 1]).then_inc(tanh_done, 1)

            def exp(s, j):
                act.wait_ge(tanh_done, s * TT + j + 2)
                tile = praw[:, j % RING, 0:T - P * j]
                nc.scalar.activation(tile, tile, ACT.Exp, scale=CAP).then_inc(exp_done, 1)

            def hi(s, j):
                act.wait_ge(mask_done, s * TT + j + 1)
                act.wait_ge(pv_done, s * TT + j + 1)
                copy_hi(prob[0][:, j % RING, 0:T - P * j], praw[:, j % RING, 0:T - P * j]).then_inc(phi_done, 1)

            def output_hi(s):
                act.wait_ge(pv_done, s * TT + TT + RING)
                copy_hi(oT[0][:, :], ps[:, 4:6, :].rearrange("p k n -> p (k n)")).then_inc(ohi_done, 1)

            def step(hd, b, old=True, new=True):
                h, s = hd.h, hd.h * B + b
                if new:
                    projected("q", 1 - b, *hd.unit(b, "q1"))
                if old:
                    hi(s - 1, 7)
                tanh(s, b, 0)
                if new:
                    projected("k0", 1 - b, *hd.unit(b, "k0"))
                    projected("k1", 1 - b, *hd.unit(b, "k1"))
                tanh(s, b, 1)
                if old:
                    output_hi(s - 1)
                exp(s, 0)
                exp(s, 1)
                tanh(s, b, 2)
                tanh(s, b, 3)
                hi(s, 0)
                hi(s, 1)
                exp(s, 2)
                exp(s, 3)
                if new:
                    projected("v0", 1 - b, *hd.unit(b, "v0"))
                tanh(s, b, 4)
                hi(s, 2)
                exp(s, 4)
                hi(s, 3)
                if new:
                    projected("v1", 1 - b, *hd.unit(b, "v1"))
                tanh(s, b, 5)
                tanh(s, b, 6)
                exp(s, 5)
                hi(s, 4)
                hi(s, 5)
                tanh(s, b, 7)
                exp(s, 6)
                exp(s, 7)
                hi(s, 6)

            first, last = Head(0, "first"), Head(H - 1, "last")
            step(first, 0, old=False)
            step(first, 1)
            with act.Fori(1, H - 1) as h:
                for b in range(B):
                    step(Head(h, "middle"), b)
            step(last, 0)
            step(last, 1, new=False)
            s = B * H
            hi(s - 1, 7)
            output_hi(s - 1)

            act.wait_ge(pj_free, UNITS_ALL)
            for n in range(2 * NT // 4):
                act.wait_ge(x1t_done, n + 1)
                nc.scalar.activation(x1T[:, n % KC, 512 * (n // KC):512 * (n // KC) + 512], ps[:, n % 2, :], ACT.Copy).then_inc(x1t_read, 1)

            def shared_halves(n):
                fn = SFC[n % 3][1]
                act.wait_ge(gu_done, n + 1)
                if n >= SR:
                    act.wait_ge(act_done, n - SR + 1)
                nc.scalar.activation(silu_s[0:fn, n % SR, :], ps[0:fn, 4 + 2 * (n % 2), :], ACT.Silu)
                nc.scalar.activation(up_s[0:fn, n % SR, :], ps[0:fn, 5 + 2 * (n % 2), :], ACT.Copy).then_inc(gu_read, 1)

            for n in range(2):
                shared_halves(n)
            act.wait_ge(diff_done, 1)
            nc.scalar.activation(wts[:, :, :], wts[:, :, :], ACT.Exp).then_inc(e_done, 1)
            for n in range(2, SHARED_UNITS):
                shared_halves(n)
            for i in range(NT):
                act.wait_ge(sd_done, i + 1)
                if i >= 4:
                    act.wait_ge(sd_added, i - 3)
                nc.scalar.activation(sdown[:, i % 4, :], ps[:, 4 + i % 2, 0:D], ACT.Copy).then_inc(sd_read, 1)

            def expert_silu(g, k):
                act.wait_ge(egu_done, g * EB + k + 1)
                nc.scalar.activation(silE[0:FH, k % 2, :], ps[0:FH, 4 + k % 2, 0:2 * C], ACT.Silu).then_inc(esil_done, 1)

            def expert_out(g, k):
                act.wait_ge(ey_done, g * EB + k + 1)
                act.wait_ge(yb_in[k % 4], g * YB_TURN[k % 4] + YB_BEFORE[k] + 1)
                nc.scalar.activation(ye[0:C, k % 4, :], ps[0:C, 6 + k % 2, 0:D], ACT.Copy).then_inc(ey_evac, 1)
                act.wait_ge(ey_evac, g * EB + k + 3)
                for r0, p0, ch, rows in expert_pieces(k):
                    act.dma_start(ybuf[p0:p0 + rows, bass.ds(g * ECH + ch, 1), :].rearrange("p o d -> p (o d)"),
                                  ye[r0:r0 + rows, k % 4, :]).then_inc(yb_in[k % 4], 16)

            expert_silu(0, 0)
            with act.Fori(0, TURNS - 1) as g:
                for k in range(EB):
                    expert_silu(g + (k + 1) // EB, (k + 1) % EB)
                    expert_out(g, k)
            for k in range(EB):
                if k + 1 < EB:
                    expert_silu(TURNS - 1, k + 1)
                expert_out(TURNS - 1, k)
            for i in range(NT):
                act.wait_ge(norm_done, i + 1)
                act.dma_start(out_v[:, i, :], yacc[:, i, :]).then_inc(out_done, 16)

        @block.gpsimd
        def _(pool):
            nc.gpsimd.memset(ones[:, :], 1.0).then_inc(consts, 1)
            nc.gpsimd.memset(mhalf[:, :], -0.5).then_inc(consts, 1)
            nc.gpsimd.memset(causal[:, :], 1.0).then_inc(consts, 1)
            pool.wait_ge(consts, 3)
            nc.gpsimd.affine_select(out=causal[:, :], in_=causal[:, :], compare_op=ALU.is_ge, fill=0.0, base=0,
                                    pattern=[[1, P]], channel_multiplier=-1).then_inc(consts, 1)
            nc.gpsimd.memset(ident[:, :], 0.0).then_inc(consts, 1)
            nc.gpsimd.memset(tri[:, :], 1.0).then_inc(consts, 1)
            nc.gpsimd.memset(onesb[:, :], 1.0).then_inc(consts, 1)
            nc.gpsimd.memset(slotsel[:, :], 0.0).then_inc(consts, 1)
            nc.gpsimd.iota(iota48[:, :], pattern=[[1, C]], base=0, channel_multiplier=0,
                           allow_small_or_imprecise_dtypes=True).then_inc(consts, 1)
            pool.wait_ge(consts, 9)
            nc.gpsimd.affine_select(out=ident[:, :], in_=ident[:, :], compare_op=ALU.not_equal, fill=1.0, base=0,
                                    pattern=[[1, P]], channel_multiplier=-1).then_inc(consts, 1)
            nc.gpsimd.affine_select(out=tri[:, :], in_=tri[:, :], compare_op=ALU.is_gt, fill=0.0, base=0,
                                    pattern=[[1, P]], channel_multiplier=-1).then_inc(consts, 1)
            nc.gpsimd.memset(slotsel[0:3 * E, 0:1], 1.0).then_inc(consts, 1)
            rest = slotsel[3 * E:NI, :]
            for row, col, value in ((0, 1, 1.0), (1, 1, float(P)), (2, 2, 1.0)):
                pool.wait_ge(consts, 12 + row)
                nc.gpsimd.affine_select(out=rest[:, col:col + 1], in_=rest[:, col:col + 1], compare_op=ALU.not_equal, fill=value,
                                 base=-row, pattern=[[0, 1]], channel_multiplier=1).then_inc(consts, 1)
            pool.wait_ge(consts, CONSTS - 2 * BLK)
            nc.gpsimd.memset(fold[:, :], 0.0).then_inc(consts, 1)
            for k in range(1 - BLK, BLK):
                pool.wait_ge(consts, CONSTS - BLK + k)
                nc.gpsimd.affine_select(out=fold[:, :], in_=fold[:, :], compare_op=ALU.not_equal, fill=1.0, base=-32 * k,
                                    pattern=[[-1, P]], channel_multiplier=1).then_inc(consts, 1)
            pool.wait_ge(consts, CONSTS)
            pool.wait_ge(g_done, 5)

            def rms(b, count):
                pool.wait_ge(pj_free, count)
                nc.gpsimd.tensor_tensor(rstd[:, b, :], var[:, b, :], mhalf[:, :], ALU.pow).then_inc(r_done, 1)

            pool.sem_inc(pacc_done, RING)
            nc.gpsimd.tensor_copy(gcur[:, :], ghead[:, 0:1]).then_inc(gcur_done, 1)
            rms(0, PROLOGUE.index("ss") + 1)

            def tile(s, b, j):
                t = s * TT + j
                pool.wait_ge(exp_done, t + 1)
                diag = praw[:, j % RING, 0:P]
                nc.gpsimd.tensor_tensor(diag, diag, causal[:, :], ALU.mult).then_inc(mask_done, 1)
                pool.wait_ge(mask_done, t + 1)
                raw = praw[:, j % RING, 0:T - P * j]
                if j == 0:
                    pool.sem_inc(waited, 1)
                    nc.gpsimd.tensor_copy(pacc[:, b, 0:P], raw[:, 0:P]).then_inc(pacc_done, 1)
                else:
                    before = praw[:, 0, P:T] if j == 1 else pacc[:, b, P * j:T]
                    pool.wait_ge(pacc_done, t + RING)
                    nc.gpsimd.tensor_tensor(pacc[:, b, P * j:T], before, raw, ALU.add).then_inc(pacc_done, 1)

            def next_head_weight(h, s):
                pool.wait_ge(qf_done, s + 1)
                pool.sem_inc(waited, 1)
                nc.gpsimd.tensor_copy(gcur[:, :], ghead[:, bass.ds(h + 1, 1)]).then_inc(gcur_done, 1)

            def step(hd, b, old=True, new=True):
                h, s = hd.h, hd.h * B + b
                if new:
                    if b == 1:
                        next_head_weight(h, s)
                if old:
                    tile(s - 1, 1 - b, 6)
                    tile(s - 1, 1 - b, 7)
                tile(s, b, 0)
                tile(s, b, 1)
                if new:
                    rms(1 - b, hd.unit(b, "ss")[0])
                tile(s, b, 2)
                tile(s, b, 3)
                tile(s, b, 4)
                tile(s, b, 5)

            first, last = Head(0, "first"), Head(H - 1, "last")
            step(first, 0, old=False)
            step(first, 1)
            with pool.Fori(1, H - 1) as h:
                for b in range(B):
                    step(Head(h, "middle"), b)
            step(last, 0)
            step(last, 1, new=False)
            tile(B * H - 1, 1, 6)
            tile(B * H - 1, 1, 7)

            def layernorm_rstd(b):
                pool.wait_ge(var1, b + 1)
                nc.gpsimd.tensor_tensor(lnr[:, TT * b:TT * b + TT], lnv[:, TT * b:TT * b + TT], mhalf[:, 0:TT], ALU.pow).then_inc(rln1, 1)

            layernorm_rstd(0)
            pool.wait_ge(pj_free, UNITS_ALL)
            for t in (sel, *cum):
                nc.gpsimd.memset(t[:, 0:PAD, :], 0.0).then_inc(pads, 1)
            nc.gpsimd.memset(grp[:, :, G:G + 5], NEG).then_inc(pads, 1)
            nc.gpsimd.memset(mk[:, :, E:E + 2], NEG).then_inc(pads, 1)
            layernorm_rstd(1)
            nc.gpsimd.iota(iota128[:, :], pattern=[[1, P]], base=0, channel_multiplier=0,
                                  allow_small_or_imprecise_dtypes=True).then_inc(pads, 1)
            nc.gpsimd.memset(emask[:, :], 1.0).then_inc(pads, 1)
            nc.gpsimd.iota(tile0[:, :, :], pattern=[[P, NT], [0, SC]], base=0, channel_multiplier=0,
                           allow_small_or_imprecise_dtypes=True).then_inc(pads, 1)
            nc.gpsimd.iota(info[:, :, 3 * E:3 * E + 1], pattern=[[0, NT], [0, 1]], base=0, channel_multiplier=1,
                           allow_small_or_imprecise_dtypes=True).then_inc(pads, 1)
            nc.gpsimd.iota(info[:, :, 3 * E + 1:3 * E + 2], pattern=[[1, NT], [0, 1]], base=0, channel_multiplier=0,
                           allow_small_or_imprecise_dtypes=True).then_inc(pads, 1)
            nc.gpsimd.memset(info[:, :, 3 * E + 2:3 * E + 4], 1.0).then_inc(pads, 1)
            pool.wait_ge(pads, 11)
            for part in range(3):
                rows = emask[E * part:E * part + E, :].rearrange("p (e c) -> p e c", c=C)
                nc.gpsimd.affine_select(out=rows, in_=rows, compare_op=ALU.is_equal, fill=0.0, base=0,
                                    pattern=[[1, E], [0, C]], channel_multiplier=-1).then_inc(pads, 1)

            pool.wait_ge(pads, 14)

            def shared_product(n):
                c, fn, tc = n % 3, SFC[n % 3][1], n // 3
                pool.wait_ge(gu_read, n + 1)
                nc.gpsimd.tensor_tensor(actS[0:fn, c, 512 * tc:512 * tc + 512], silu_s[0:fn, n % SR, :], up_s[0:fn, n % SR, :],
                                        ALU.mult).then_inc(act_done, 1)

            def apart(i):
                nc.gpsimd.tensor_tensor(onehot[:, i, :].rearrange("p (e c) -> p e c", c=C),
                                        posb[:, i, :].unsqueeze(2).to_broadcast([P, E, C]),
                                        iota48[:, :].unsqueeze(1).to_broadcast([P, E, C]), ALU.subtract).then_inc(apart_done, 1)

            for n in range(SHARED_FIRST):
                shared_product(n)
            pool.wait_ge(posb_done, 1)
            for k in range(len(HELPED)):
                apart(HELPED[k])
                if SHARED_FIRST + k <= SHARED_SECOND:
                    shared_product(SHARED_FIRST + k)
            for n in range(SHARED_FIRST + len(HELPED), SHARED_SECOND + 1):
                shared_product(n)
            pool.wait_ge(tok_done, 1)
            pool.wait_ge(x1_out, 16 * B)

            def gather(m):
                nc.gpsimd.indirect_dma_start(xg[:, m, :], None, x1_d, bass.IndirectOffsetOnAxis(ap=toki[:, m:m + 1], axis=0)).then_inc(xg_in[m // 4], 16)

            def add_shared(i):
                pool.wait_ge(sd_read, i + 1)
                nc.gpsimd.tensor_tensor(yacc[:, i, :], yacc[:, i, :], sdown[:, i % 4, :], ALU.add).then_inc(sd_added, 1)

            for m in range(SC):
                gather(m)
                if m >= 4:
                    add_shared(m - 4)
            for n in range(SHARED_SECOND + 1, SHARED_UNITS):
                shared_product(n)
            for i in range(SC - 4, NT):
                add_shared(i)
            for i in range(NT):
                pool.wait_ge(var2, i + 1)
                nc.gpsimd.tensor_tensor(lnr[:, i:i + 1], lnv[:, i:i + 1], mhalf[:, 0:1], ALU.pow).then_inc(rln2, 1)

        @block.vector
        def _(dve):
            v = nc.vector
            dve.sem_inc(o_evac, 1)
            dve.sem_inc(eact_done, 2)
            dve.sem_inc(plo_done, RING)

            def lo_of(dst, x_, hi, done):
                v.tensor_tensor(dst, x_, hi.bitcast(F32), ALU.subtract).then_inc(done, 1)

            ALL = slice(None)

            def split_x(b):
                cols = slice(b * T, b * T + T)
                lo_of(xT[1][:, :, cols], xraw[:, :, cols], xT[0][:, :, cols], xlo_done)

            def split(pair_, at_, src, hi_sem, n, lo_sem):
                v.tensor_copy(pair_[0][at_], src).then_inc(hi_sem, 1)
                dve.wait_ge(hi_sem, n)
                lo_of(pair_[1][at_], src, pair_[0][at_], lo_sem)

            dve.wait_ge(w_in, 16)
            split(wqk, (ALL,) * 4, wraw[:, :, :, :], whi_done, 1, wlo_done)
            dve.wait_ge(xhi_done, 1)
            split_x(0)
            dve.wait_ge(small_in, 64)
            v.tensor_tensor(gtmp[:, 2, :], gtmp[:, 0, :], gtmp[:, 0, :], ALU.mult).then_inc(g_done, 1)
            v.tensor_tensor(gtmp[:, 3, :], gtmp[:, 1, :], gtmp[:, 1, :], ALU.mult).then_inc(g_done, 1)
            v.tensor_tensor(nrm[:, 2, :], nrm[:, 0, :], nrm[:, 1, :], ALU.mult).then_inc(g_done, 1)
            dve.wait_ge(g_done, 3)
            v.tensor_tensor(gtmp[:, 2, :], gtmp[:, 2, :], gtmp[:, 3, :], ALU.add).then_inc(g_done, 1)
            dve.wait_ge(g_done, 4)
            v.tensor_scalar(ghead[:, :], gtmp[:, 2, :], nrm[:, 2, :], DH ** -0.5 / CAP, ALU.mult, ALU.mult).then_inc(g_done, 1)
            dve.wait_ge(xhi_done, 2)
            split_x(1)
            dve.wait_ge(x_in, 16)

            def projected(what, b, step, count, bank_no):
                dve.wait_ge(pj_done, count)
                bank = ps[:, bank_no, :]
                if what == "ss":
                    for g in range(BLK):
                        rows = slice(32 * g, 32 * g + 32)
                        last = v.tensor_scalar(var[rows, b, :].rearrange("p (m j) -> p m j", m=2),
                                               bank[rows, 0:2 * BLK * TT].rearrange("p (m g j) -> p m g j", m=2, g=BLK)[:, :, g, :],
                                               1.0 / DH, RMS_EPS, ALU.mult, ALU.add)
                    last.then_inc(pj_free, 1)
                    return
                cols = slice(512 * int(what[1]), 512 * int(what[1]) + 512)
                if what[0] == "q":
                    if what == "q0" and not (isinstance(step, int) and step == 0):
                        dve.wait_ge(qlo_done, step)
                    v.tensor_copy(qraw[:, cols], bank).then_inc(pj_free, 1)
                    return
                dve.wait_ge(kvhi_done, step * 4 + ["k0", "k1", "v0", "v1"].index(what) + 1)
                dst = kT if what[0] == "k" else vS
                lo_of(dst[1][:, b, cols], bank, dst[0][:, b, cols], pj_free)

            def fold_squares(step, half):
                n, cols = half % 2, slice(T // 2 * (half % 2), T // 2 * (half % 2) + T // 2)
                if half < 2:
                    dve.wait_ge(qsq_done, step + 1)
                    src, g, j = qsq[:, cols].rearrange("d (g t j) -> d g j t", t=32, j=TT), BLK // 2, TT
                    dst = sqp[:, 0, g * n:g * n + g, :]
                    blocks = sqT[:, :].rearrange("d (g j t) -> d g j t", g=g, j=j)
                    summed_ = blocks
                else:
                    dve.wait_ge(ksq_done, step * 2 + n + 1)
                    g, j = BLK, TT // 2
                    src = ksq[:, cols].rearrange("d (j g t) -> d j g t", g=g, t=32)
                    dst = sqp[:, 1, :, j * n:j * n + j]
                    blocks = sqT[:, :].rearrange("d (j g t) -> d j g t", j=j, g=g)
                    summed_ = sqT[:, :].rearrange("d (j g t) -> d g j t", j=j, g=g)
                count = step * 8 + half * 2
                if not (isinstance(count, int) and count == 0):
                    dve.wait_ge(folded, count)
                v.transpose(blocks, src).then_inc(folded, 1)
                dve.wait_ge(folded, count + 1)
                v.tensor_reduce(dst, summed_, AX, ALU.add).then_inc(folded, 1)

            def scale_queries(step, b):
                dve.wait_ge(rqB_in, step * 16 + 16)
                v.scalar_tensor_tensor(qraw[:, :], qraw[:, :], gcur[:, :], rqB[:, :], ALU.mult, ALU.mult).then_inc(qf_done, 1)
                dve.wait_ge(qf_done, step + 1)
                split(qhat, (ALL, b, ALL), qraw[:, :], qhi_done, step + 1, qlo_done)

            for n, what in enumerate(PROLOGUE):
                if what == "k0":
                    fold_squares(0, 0)
                    fold_squares(0, 1)
                if what == "v0":
                    fold_squares(0, 2)
                    fold_squares(0, 3)
                projected(what, 0, 0, n + 1, PJ + n % 2)
            dve.wait_ge(gcur_done, 1)
            scale_queries(0, 0)

            def tile(s, j):
                dve.wait_ge(phi_done, s * TT + j + 1)
                n = T - P * j
                lo_of(prob[1][:, j % RING, 0:n], praw[:, j % RING, 0:n], prob[0][:, j % RING, 0:n], plo_done)

            def out_projected(b, u, sums_count, count, bank_no):
                if u == 0:
                    dve.wait_ge(pj_free, sums_count)
                dve.wait_ge(pj_done, count)
                for i in range(2):
                    y = yacc[:, b * TT + 2 * u + i, :]
                    last = v.scalar_tensor_tensor(y, ps[:, bank_no, D * i:D * i + D], rsum[:, b, 2 * u + i:2 * u + i + 1], y,
                                                  ALU.mult, ALU.add)
                last.then_inc(pj_free, 1)

            def output_lo(s):
                dve.wait_ge(ohi_done, s + 1)
                lo_of(oT[1][:, :], ps[:, 4:6, :].rearrange("p k n -> p (k n)"), oT[0][:, :], o_evac)

            def summed(b, count, bank_no):
                dve.wait_ge(pj_done, count)
                v.reciprocal(rsum[:, b, :], ps[:, bank_no, 0:TT]).then_inc(pj_free, 1)

            def split_output_weights(hd):
                dve.wait_ge(wo_in, hd.h * 16 + 16)
                if not hd.first:
                    dve.wait_ge(pj_done, hd.unit(0, "op3")[0])
                split(wo, (ALL, ALL), woraw[:, :], wohi_done, hd.h + 1, wolo_done)

            def split_next_weights(hd):
                dve.wait_ge(w_in, hd.h * 16 + 32)
                dve.wait_ge(pj_done, hd.unit(0, "k1")[0])
                split(wqk, (ALL,) * 4, wraw[:, :, :, :], whi_done, hd.h + 2, wlo_done)

            def step(hd, b, old=True, new=True):
                h, s = hd.h, hd.h * B + b
                if b == 1:
                    split_output_weights(hd)
                if new:
                    projected("q0", 1 - b, s + 1, *hd.unit(b, "q0"))
                    projected("q1", 1 - b, s + 1, *hd.unit(b, "q1"))
                if old:
                    tile(s - 1, 4)
                    tile(s - 1, 5)
                    tile(s - 1, 6)
                if new:
                    fold_squares(s + 1, 0)
                if old:
                    tile(s - 1, 7)
                if new:
                    fold_squares(s + 1, 1)
                    projected("k0", 1 - b, s + 1, *hd.unit(b, "k0"))
                    fold_squares(s + 1, 2)
                    if b == 0 and not hd.last:
                        split_next_weights(hd)
                    projected("k1", 1 - b, s + 1, *hd.unit(b, "k1"))
                if old:
                    output_lo(s - 1)
                if new:
                    fold_squares(s + 1, 3)
                if old:
                    summed(1 - b, *hd.unit(b, "sums"))
                    out_projected(1 - b, 0, hd.unit(b, "sums")[0], *hd.unit(b, "op0"))
                if new:
                    projected("ss", 1 - b, s + 1, *hd.unit(b, "ss"))
                tile(s, 0)
                if old:
                    out_projected(1 - b, 1, hd.unit(b, "sums")[0], *hd.unit(b, "op1"))
                tile(s, 1)
                if new:
                    projected("v0", 1 - b, s + 1, *hd.unit(b, "v0"))
                if old:
                    out_projected(1 - b, 2, hd.unit(b, "sums")[0], *hd.unit(b, "op2"))
                tile(s, 2)
                if old:
                    out_projected(1 - b, 3, hd.unit(b, "sums")[0], *hd.unit(b, "op3"))
                tile(s, 3)
                if new:
                    projected("v1", 1 - b, s + 1, *hd.unit(b, "v1"))
                    if b == 0:
                        dve.sem_inc(wv_free, 1)
                    if b == 1:
                        dve.wait_ge(gcur_done, h + 2)
                    scale_queries(s + 1, 1 - b)

            first, last = Head(0, "first"), Head(H - 1, "last")
            step(first, 0, old=False)
            step(first, 1)
            with dve.Fori(1, H - 1) as h:
                for b in range(B):
                    step(Head(h, "middle"), b)
            step(last, 0)
            step(last, 1, new=False)

            steps = [0]

            def counted(ins):
                steps[0] += 1
                ins.then_inc(dstep, 1)

            def settle():
                dve.wait_ge(dstep, steps[0])

            def tile_stats(i0, i1):
                for i in range(i0, i1):
                    counted(v.bn_stats(stats[:, i, :], yacc[:, i, :]))

            def layernorm_stats(b):
                settle()
                for i in range(TT * b, TT * b + TT):
                    counted(v.bn_aggr(mv[:, i, :], stats[:, i, :]))
                settle()
                v.tensor_scalar(lnv[:, TT * b:TT * b + TT], mv[:, TT * b:TT * b + TT, 1], LN_EPS, None, ALU.add).then_inc(var1, 1)

            def normalise(i):
                return v.tensor_scalar(yacc[:, i, :], yacc[:, i, :], mv[:, i, 0:1], lnr[:, i:i + 1], ALU.subtract, ALU.mult)

            end, s = Head(H, "tail"), B * H
            dve.wait_ge(pj_free, last.unit(1, "op3")[0])
            for n, j in enumerate((4, 5, 6, 7)):
                tile(s - 1, j)
                tile_stats(TT * n // 4, TT * (n + 1) // 4)
            output_lo(s - 1)
            layernorm_stats(0)
            summed(1, *end.unit(0, "sums"))
            for u in range(4):
                out_projected(1, u, end.unit(0, "sums")[0], *end.unit(0, f"op{u}"))
            dve.wait_ge(pj_free, UNITS_ALL)
            for b in range(B):
                if b:
                    tile_stats(TT * b, TT * b + TT)
                    layernorm_stats(b)
                dve.wait_ge(rln1, b + 1)
                for i in range(TT * b, TT * b + TT):
                    ins = normalise(i)
                ins.then_inc(x1_done, 1)

            dve.wait_ge(consts, CONSTS)
            dve.wait_ge(pads, 5)
            dve.wait_ge(logit_done, 1)
            counted(v.tensor_copy(lg[:, :, :].rearrange("p i e -> p (i e)"), ps[:, 2, :]))
            settle()
            counted(v.tensor_reduce(grp[:, :, 0:G], lg[:, :, :].rearrange("p i (g e) -> p i g e", e=EG), AX, ALU.max))
            settle()
            for i in range(NT):
                counted(v.max(g8[:, i, :], grp[:, i, 0:G]))
            settle()
            counted(v.memset(g8[:, :, TOPG:8], NEG))
            settle()
            for i in range(NT):
                counted(v.match_replace(grep[:, i, :], g8[:, i, :], grp[:, i, :], POS))
            settle()
            counted(v.tensor_tensor(keep[:, :, :], grep[:, :, 0:G], grp[:, :, 0:G], ALU.not_equal))
            settle()
            counted(v.tensor_tensor(lg[:, :, :].rearrange("p i (g e) -> p (i g) e", e=EG),
                                 lg[:, :, :].rearrange("p i (g e) -> p (i g) e", e=EG),
                                 keep[:, :, :].rearrange("p i g -> p (i g)").unsqueeze(2).to_broadcast([P, NT * G, EG]), ALU.mult))
            settle()
            counted(v.tensor_scalar(mk[:, :, 0:E], lg[:, :, :], 0.0, None, ALU.add))
            settle()
            for i in range(NT):
                counted(v.max(m8[:, i, :], mk[:, i, 0:E]))
            settle()
            v.tensor_tensor(wts[:, :, :], mk[:, :, 0:E], m8[:, :, 0:1].to_broadcast([P, NT, E]), ALU.subtract).then_inc(diff_done, 1)
            dve.wait_ge(diff_done, 1)
            counted(v.memset(m8[:, :, TOPK:8], NEG))
            settle()
            for i in range(NT):
                counted(v.match_replace(mrep[:, i, :], m8[:, i, :], mk[:, i, :], POS))
            settle()
            counted(v.tensor_tensor(sel[:, PAD:PAD + NT, :], mrep[:, :, 0:E], mk[:, :, 0:E], ALU.not_equal))
            src = sel
            for k, span in enumerate((1, 2, 4, 8)):
                settle()
                dst = cum[k % 2]
                ins = v.tensor_tensor(dst[:, PAD:PAD + NT, :], src[:, PAD:PAD + NT, :], src[:, PAD - span:PAD + NT - span, :], ALU.add)
                src = dst
                if span < 8:
                    counted(ins)
            ins.then_inc(sel_done, 1)
            counted(v.tensor_scalar(posm[:, :, :], sel[:, PAD:PAD + NT, :], -4096.0, 4096.0, ALU.mult, ALU.add))
            dve.wait_ge(pos_done, 1)
            settle()
            v.tensor_tensor(posb[:, :, :].rearrange("p i e -> p (i e)"), posm[:, :, :].rearrange("p i e -> p (i e)"), ps[:, 3, :], ALU.add).then_inc(posb_done, 1)
            dve.wait_ge(pads, 14)
            dve.wait_ge(e_done, 1)
            counted(v.tensor_reduce(srow[:, :], wts[:, :, :], AX, ALU.add))
            settle()
            counted(v.reciprocal(rrow[:, :], srow[:, :]))
            settle()
            counted(v.tensor_scalar(rrow[:, :], rrow[:, :], ROUTE_SCALE, None, ALU.mult))

            def place(i):
                if i in HELPED:
                    dve.wait_ge(apart_done, HELPED.index(i) + 1)
                    v.tensor_scalar(onehot[:, i, :], onehot[:, i, :], 0.0, None, ALU.is_equal).then_inc(onehot_done, 1)
                    return
                v.tensor_tensor(onehot[:, i, :].rearrange("p (e c) -> p e c", c=C),
                                posb[:, i, :].unsqueeze(2).to_broadcast([P, E, C]),
                                iota48[:, :].unsqueeze(1).to_broadcast([P, E, C]), ALU.is_equal).then_inc(onehot_done, 1)

            dve.wait_ge(posb_done, 1)
            place(0)
            settle()
            counted(v.tensor_tensor(wts[:, :, :], wts[:, :, :], rrow[:, :].unsqueeze(2).to_broadcast([P, NT, E]), ALU.mult))
            place(1)
            settle()
            counted(v.tensor_copy(info[:, :, 0:E], wts[:, :, :]))
            place(2)
            settle()
            counted(v.tensor_tensor(wrest[:, :, :], wts[:, :, :], info[:, :, 0:E], ALU.subtract))
            place(3)
            settle()
            counted(v.tensor_copy(info[:, :, E:2 * E], wrest[:, :, :]))
            place(4)
            settle()
            counted(v.tensor_tensor(wrest[:, :, :], wrest[:, :, :], info[:, :, E:2 * E], ALU.subtract))
            place(5)
            settle()
            v.tensor_copy(info[:, :, 2 * E:3 * E], wrest[:, :, :]).then_inc(info_in, 1)
            for i in range(6, NT):
                place(i)
            dve.wait_ge(infot_done, 1)
            for q in range(3):
                v.tensor_tensor(minfo[0:NI, 512 * q:512 * q + 512], ps[0:NI, q, :], emask[0:NI, 512 * q:512 * q + 512],
                                ALU.mult).then_inc(minfo_done, 1)
            dve.wait_ge(slot_done, 1)
            slot = ps[:, 3, 0:3 * SC].rearrange("p (m n) -> p m n", n=3)
            v.tensor_copy(toki[:, :], slot[:, :, 1]).then_inc(tok_done, 1)
            counted(v.tensor_scalar(tok[:, :], slot[:, :, 2], -1.0, None, ALU.add))
            counted(v.tensor_copy(wslot[:, :], slot[:, :, 0]))
            settle()
            counted(v.tensor_tensor(tok[:, :], tok[:, :], slot[:, :, 1], ALU.add))
            settle()
            v.tensor_tensor(tokc[:, :, :], tok[:, :].unsqueeze(1).to_broadcast([P, NT, SC]), tile0[:, :, :], ALU.subtract).then_inc(tokc_done, 1)
            for n in range(3 * KC):
                q, c = n // KC, n % KC
                dve.wait_ge(xbt_done, n + 1)
                v.tensor_copy(xbT[:, c, 512 * q:512 * q + 512], ps[:, n % 2, :]).then_inc(xbt_read, 1)

            def product(g, k):
                dve.wait_ge(esil_done, g * EB + k + 1)
                v.tensor_tensor(actE[0:FH, k % 2].rearrange("p k c -> p (k c)"), silE[0:FH, k % 2, :],
                                ps[0:FH, 4 + k % 2, 2 * C:4 * C], ALU.mult).then_inc(eact_done, 1)

            def rows(t, g, m=None):
                return t[:, bass.ds(g * ECH, ECH), :] if m is None else t[:, bass.ds(g * ECH + m, 1), :]

            def weight(g, m):
                row = rows(ybuf, g, m).rearrange("p o d -> p (o d)")
                v.tensor_scalar(row, row, wslot[:, bass.ds(g * ECH + m, 1)], None, ALU.mult).then_inc(yw_done, 1)

            def weighted_hi(g):
                dve.wait_ge(yw_done, g * ECH + ECH)
                v.tensor_copy(rows(y_hi, g), rows(ybuf, g)).then_inc(yhi_done, 1)

            def weighted_lo(g):
                dve.wait_ge(yhi_done, g + 1)
                lo_of(rows(y_lo, g), rows(ybuf, g), rows(y_hi, g), ylo_done)

            def landed(g):
                for s in range(4):
                    dve.wait_ge(yb_in[s], g * YB_TURN[s] + (YB_TURN[s] + 1))

            def tokens_of_slots(g, k):
                i, m0 = g * (EB // 2) + k // 2, SC // 2 * (k % 2)
                half = SC // 2
                v.tensor_tensor(ohT[:, bass.ds(i, 1), m0:m0 + half, :].rearrange("p o m t -> p (o m) t"),
                                tokc[:, bass.ds(i, 1), m0:m0 + half].rearrange("p o m -> p (o m)").unsqueeze(2).to_broadcast([P, half, P]),
                                iota128[:, :].unsqueeze(1).to_broadcast([P, half, P]), ALU.is_equal).then_inc(oht_done, 1)

            dve.wait_ge(sd_added, NT)
            dve.wait_ge(tokc_done, 1)
            for k in range(EB):
                product(0, k)
                tokens_of_slots(0, k)
            with dve.Fori(1, TURNS) as g:
                for k in range(EB):
                    product(g, k)
                    tokens_of_slots(g, k)
                    if k == 2:
                        landed(g - 1)
                    if 2 <= k < 2 + ECH:
                        weight(g - 1, k - 2)
                    if k == 5:
                        weighted_hi(g - 1)
                    if k == 6:
                        weighted_lo(g - 1)
            landed(TURNS - 1)
            for m in range(ECH):
                weight(TURNS - 1, m)
            weighted_hi(TURNS - 1)
            weighted_lo(TURNS - 1)

            for i in range(NT + 2):
                if i < NT:
                    dve.wait_ge(comb_done, i + 1)
                    v.tensor_tensor(yacc[:, i, :], yacc[:, i, :], ps[:, i % 4, 0:D], ALU.add).then_inc(comb_free, 1)
                if i >= 2:
                    dve.wait_ge(rln2, i - 1)
                    normalise(i - 2).then_inc(norm_done, 1)
                if i < NT:
                    dve.wait_ge(comb_free, i + 1)
                    counted(v.bn_stats(stats[:, i, :], yacc[:, i, :]))
                    settle()
                    counted(v.bn_aggr(mv[:, i, :], stats[:, i, :]))
                    settle()
                    v.tensor_scalar(lnv[:, i:i + 1], mv[:, i, 1:2], LN_EPS, None, ALU.add).then_inc(var2, 1)


def _yb_counts():
    turn, at_ = [0] * 4, []
    for k in range(EB):
        pieces = 1 + ((k * C) // P != ((k + 1) * C - 1) // P)
        at_.append(turn[k % 4])
        turn[k % 4] += 16 * pieces
    return turn, at_


YB_TURN, YB_BEFORE = _yb_counts()


def kernel(**inputs):
    import concourse.bacc as bacc
    from concourse.bass_utils import run_bass_kernel_spmd as run

    a = {n: np.asarray(v) for n, v in inputs.items()}
    x = a["L0_attn_x"].reshape(N, D)

    def heads(w):
        return w.reshape(H, DH, KC, P).transpose(0, 3, 2, 1)

    wqkv = np.stack([heads(a["L0_attn_wq"]), heads(a["L0_attn_wk"]), heads(a["L0_attn_wv"])], axis=2)
    wo = a["L0_attn_wo"].reshape(D, H, DH).transpose(1, 2, 0)

    def rope(t):
        return np.repeat(t[:H], 2, axis=1).T

    arrays = {
        "x": x, "xT": x.T, "wqkv": wqkv, "wo": wo,
        "qn": a["L0_attn_q_norm_w"].reshape(DH, 1), "kn": a["L0_attn_k_norm_w"].reshape(DH, 1),
        "cos": rope(a["L0_attn_rope_cos"]), "sin": rope(a["L0_attn_rope_sin"]),
        "gw": a["L0_ffn_gate_w"].T, "wgu": a["L0_ffn_w_gate_up"], "wd": a["L0_ffn_w_down"],
        "wsgu": a["L0_ffn_ws_gate_up"], "wsd": a["L0_ffn_ws_down"],
    }
    nc = bacc.Bacc("TRN2", target_bir_lowering=False, num_devices=1)
    feed, args = {}, []
    for name, arr in arrays.items():
        arr = np.ascontiguousarray(arr)
        feed[f"in_{name}"] = arr
        args.append(nc.dram_tensor(f"in_{name}", arr.shape, mybir.dt.from_np(arr.dtype), kind="ExternalInput").ap())
    args.append(nc.dram_tensor("out_0", (N, D), F32, kind="ExternalOutput").ap())
    block_kernel(nc, *args)
    r = run(nc, [feed], core_ids=[0])
    return r.results[0]["out_0"].reshape(B, T, D)
```
